# Optimizing a Trainium2 kernel written in Bass

```python
import numpy as np
import jax
import jax.numpy as jnp

def _softmax(x, axis=-1):
    return jax.nn.softmax(x, axis=axis)

def _gelu(x):
    return jax.nn.gelu(x, approximate=True)

def _silu(x):
    return jax.nn.silu(x)

def _sigmoid(x):
    return jax.nn.sigmoid(x)

def _layernorm(x, axis=-1, eps=1e-05):
    m = jnp.mean(x, axis=axis, keepdims=True)
    v = jnp.var(x, axis=axis, keepdims=True)
    return (x - m) / jnp.sqrt(v + eps)

def _scatter_add(tgt, idx, src, axis=0):
    return tgt.at[idx].add(src)

def _segment_sum(src, seg, n):
    return jax.ops.segment_sum(src, seg, n)
kernel_name = 'mk_seq_preln_d1_jaxref_r8_4115ca'

def setup_inputs(seed: int=0):
    np.random.seed(seed)
    _w = jnp.asarray

    def _L0_attn_setup():
        import jax, jax.numpy as jnp
        import numpy as np
        LN_EPS = 1e-05
        WKV_EPS = 1e-08
        NEG_INF = -1e+38

        def _layernorm(x, g, b):
            m = jnp.mean(x, axis=-1, keepdims=True)
            v = jnp.mean(jnp.square(x - m), axis=-1, keepdims=True)
            return (x - m) * jax.lax.rsqrt(v + LN_EPS) * g + b

        def _wkv(w, u, k, v):
            B, T, C = k.shape
            aa0 = jnp.zeros((B, C), k.dtype)
            bb0 = jnp.full((B, C), NEG_INF, k.dtype)

            def step(carry, kv_t):
                aa, bb = carry
                kk, vv = kv_t
                ww = u + kk
                p = jnp.maximum(bb, ww)
                e1 = jnp.exp(bb - p)
                e2 = jnp.exp(ww - p)
                y_t = (e1 * aa + e2 * vv) / (e1 + e2 + WKV_EPS)
                ww = w + bb
                p = jnp.maximum(ww, kk)
                e1 = jnp.exp(ww - p)
                e2 = jnp.exp(kk - p)
                aa = e1 * aa + e2 * vv
                bb = p + jnp.log(e1 + e2 + WKV_EPS)
                return ((aa, bb), y_t)
            (aa, bb), ys = jax.lax.scan(step, (aa0, bb0), (jnp.swapaxes(k, 0, 1), jnp.swapaxes(v, 0, 1)))
            y = jnp.swapaxes(ys, 0, 1)
            new_state = jnp.stack([aa, bb], axis=-1)
            return (y, new_state)

        def _reference_tuple_inner(x, time_decay, time_first, W_tm, g1, b1, tmk, tmv, tmr, W_cm, W_cp, g2, b2, cmk, cmr):
            x_prev = jnp.concatenate([x[:, :1], x[:, :-1]], axis=1)
            kvr = _layernorm(x, g1, b1) @ W_tm
            k, v, r = jnp.split(kvr, 3, axis=-1)
            k = k * tmk + x_prev * (1.0 - tmk)
            v = v * tmv + x_prev * (1.0 - tmv)
            r = jax.nn.sigmoid(r * tmr + x_prev * (1.0 - tmr))
            y, new_state = _wkv(time_decay, time_first, k, v)
            x = x + r * y
            xp = jnp.concatenate([x[:, -1:], x[:, :-1]], axis=1)
            xn = _layernorm(x, g2, b2)
            kk = xn @ W_cm
            cmk4 = jnp.tile(cmk, (1, 1, 4))
            xp4 = jnp.tile(xp, (1, 1, 4))
            kk = kk * cmk4 + xp4 * (1.0 - cmk4)
            rr = jax.nn.sigmoid(xn * cmr + xp * (1.0 - cmr))
            vv = jnp.square(jax.nn.relu(kk)) @ W_cp
            x = x + rr * vv
            return (x, new_state)
        key = jax.random.key(seed)
        ks = jax.random.split(key, 12)
        B, T, C = (8, 256, 128)
        scale = 0.02
        return {'x': jax.random.normal(ks[0], (B, T, C), jnp.float32), 'time_decay': jax.random.uniform(ks[1], (C,), jnp.float32, -1.0, 1.0), 'time_first': jax.random.uniform(ks[2], (C,), jnp.float32, -1.0, 1.0), 'W_tm': jax.random.normal(ks[3], (C, 3 * C), jnp.float32) * scale, 'g1': jnp.ones((C,), jnp.float32), 'b1': jnp.zeros((C,), jnp.float32), 'tmk': jax.random.uniform(ks[4], (1, 1, C), jnp.float32), 'tmv': jax.random.uniform(ks[5], (1, 1, C), jnp.float32), 'tmr': jax.random.uniform(ks[6], (1, 1, C), jnp.float32), 'W_cm': jax.random.normal(ks[7], (C, 4 * C), jnp.float32) * scale, 'W_cp': jax.random.normal(ks[8], (4 * C, C), jnp.float32) * scale, 'g2': jnp.ones((C,), jnp.float32), 'b2': jnp.zeros((C,), jnp.float32), 'cmk': jax.random.uniform(ks[9], (1, 1, C), jnp.float32), 'cmr': jax.random.uniform(ks[10], (1, 1, C), jnp.float32)}
    _L0_attn_in = _L0_attn_setup()

    def _L0_ffn_setup():
        import jax, jax.numpy as jnp
        import numpy as np
        H = 16
        E = 8
        EPS = 1e-05

        def _layernorm(x, g, b):
            mu = jnp.mean(x, axis=-1, keepdims=True)
            var = jnp.mean(jnp.square(x - mu), axis=-1, keepdims=True)
            return (x - mu) * jax.lax.rsqrt(var + EPS) * g + b
        key = jax.random.key(seed)
        T, B, C = (128, 8, 128)
        ks = jax.random.split(key, 12)
        s = 0.02
        return {'x': jax.random.normal(ks[0], (T, B, C), jnp.float32), 'in_proj_w': jax.random.normal(ks[1], (3 * C, C), jnp.float32) * s, 'in_proj_b': jnp.zeros((3 * C,), jnp.float32), 'out_w': jax.random.normal(ks[2], (C, C), jnp.float32) * s, 'out_b': jnp.zeros((C,), jnp.float32), 'ln1_g': jnp.ones((C,), jnp.float32), 'ln1_b': jnp.zeros((C,), jnp.float32), 'router_w': jax.random.normal(ks[3], (E, C), jnp.float32) * s, 'router_b': jnp.zeros((E,), jnp.float32), 'w1': jax.random.normal(ks[4], (E, C, C), jnp.float32) * s, 'b1': jnp.zeros((E, C), jnp.float32), 'w2': jax.random.normal(ks[5], (E, C, C), jnp.float32) * s, 'b2': jnp.zeros((E, C), jnp.float32), 'ln2_g': jnp.ones((C,), jnp.float32), 'ln2_b': jnp.zeros((C,), jnp.float32)}
    _L0_ffn_in = _L0_ffn_setup()
    _d = {'L0_attn_x': _L0_attn_in['x'], 'L0_attn_time_decay': _L0_attn_in['time_decay'], 'L0_attn_time_first': _L0_attn_in['time_first'], 'L0_attn_W_tm': _L0_attn_in['W_tm'], 'L0_attn_g1': _L0_attn_in['g1'], 'L0_attn_b1': _L0_attn_in['b1'], 'L0_attn_tmk': _L0_attn_in['tmk'], 'L0_attn_tmv': _L0_attn_in['tmv'], 'L0_attn_tmr': _L0_attn_in['tmr'], 'L0_attn_W_cm': _L0_attn_in['W_cm'], 'L0_attn_W_cp': _L0_attn_in['W_cp'], 'L0_attn_g2': _L0_attn_in['g2'], 'L0_attn_b2': _L0_attn_in['b2'], 'L0_attn_cmk': _L0_attn_in['cmk'], 'L0_attn_cmr': _L0_attn_in['cmr'], 'L0_ffn_in_proj_w': _L0_ffn_in['in_proj_w'], 'L0_ffn_in_proj_b': _L0_ffn_in['in_proj_b'], 'L0_ffn_out_w': _L0_ffn_in['out_w'], 'L0_ffn_out_b': _L0_ffn_in['out_b'], 'L0_ffn_ln1_g': _L0_ffn_in['ln1_g'], 'L0_ffn_ln1_b': _L0_ffn_in['ln1_b'], 'L0_ffn_router_w': _L0_ffn_in['router_w'], 'L0_ffn_router_b': _L0_ffn_in['router_b'], 'L0_ffn_w1': _L0_ffn_in['w1'], 'L0_ffn_b1': _L0_ffn_in['b1'], 'L0_ffn_w2': _L0_ffn_in['w2'], 'L0_ffn_b2': _L0_ffn_in['b2'], 'L0_ffn_ln2_g': _L0_ffn_in['ln2_g'], 'L0_ffn_ln2_b': _L0_ffn_in['ln2_b']}
    _x0 = _d['L0_attn_x']
    _d['L0_attn_x'] = jax.random.normal(jax.random.fold_in(jax.random.key(seed), 1), (8, 512, 128), dtype=_x0.dtype)
    del _x0
    return _d

def reference(L0_attn_x, L0_attn_time_decay, L0_attn_time_first, L0_attn_W_tm, L0_attn_g1, L0_attn_b1, L0_attn_tmk, L0_attn_tmv, L0_attn_tmr, L0_attn_W_cm, L0_attn_W_cp, L0_attn_g2, L0_attn_b2, L0_attn_cmk, L0_attn_cmr, L0_ffn_in_proj_w, L0_ffn_in_proj_b, L0_ffn_out_w, L0_ffn_out_b, L0_ffn_ln1_g, L0_ffn_ln1_b, L0_ffn_router_w, L0_ffn_router_b, L0_ffn_w1, L0_ffn_b1, L0_ffn_w2, L0_ffn_b2, L0_ffn_ln2_g, L0_ffn_ln2_b):

    def _L0_attn_ref(x, time_decay, time_first, W_tm, g1, b1, tmk, tmv, tmr, W_cm, W_cp, g2, b2, cmk, cmr):
        import jax, jax.numpy as jnp
        import numpy as np
        LN_EPS = 1e-05
        WKV_EPS = 1e-08
        NEG_INF = -1e+38

        def _layernorm(x, g, b):
            m = jnp.mean(x, axis=-1, keepdims=True)
            v = jnp.mean(jnp.square(x - m), axis=-1, keepdims=True)
            return (x - m) * jax.lax.rsqrt(v + LN_EPS) * g + b

        def _wkv(w, u, k, v):
            B, T, C = k.shape
            aa0 = jnp.zeros((B, C), k.dtype)
            bb0 = jnp.full((B, C), NEG_INF, k.dtype)

            def step(carry, kv_t):
                aa, bb = carry
                kk, vv = kv_t
                ww = u + kk
                p = jnp.maximum(bb, ww)
                e1 = jnp.exp(bb - p)
                e2 = jnp.exp(ww - p)
                y_t = (e1 * aa + e2 * vv) / (e1 + e2 + WKV_EPS)
                ww = w + bb
                p = jnp.maximum(ww, kk)
                e1 = jnp.exp(ww - p)
                e2 = jnp.exp(kk - p)
                aa = e1 * aa + e2 * vv
                bb = p + jnp.log(e1 + e2 + WKV_EPS)
                return ((aa, bb), y_t)
            (aa, bb), ys = jax.lax.scan(step, (aa0, bb0), (jnp.swapaxes(k, 0, 1), jnp.swapaxes(v, 0, 1)))
            y = jnp.swapaxes(ys, 0, 1)
            new_state = jnp.stack([aa, bb], axis=-1)
            return (y, new_state)

        def _reference_tuple_inner(x, time_decay, time_first, W_tm, g1, b1, tmk, tmv, tmr, W_cm, W_cp, g2, b2, cmk, cmr):
            x_prev = jnp.concatenate([x[:, :1], x[:, :-1]], axis=1)
            kvr = _layernorm(x, g1, b1) @ W_tm
            k, v, r = jnp.split(kvr, 3, axis=-1)
            k = k * tmk + x_prev * (1.0 - tmk)
            v = v * tmv + x_prev * (1.0 - tmv)
            r = jax.nn.sigmoid(r * tmr + x_prev * (1.0 - tmr))
            y, new_state = _wkv(time_decay, time_first, k, v)
            x = x + r * y
            xp = jnp.concatenate([x[:, -1:], x[:, :-1]], axis=1)
            xn = _layernorm(x, g2, b2)
            kk = xn @ W_cm
            cmk4 = jnp.tile(cmk, (1, 1, 4))
            xp4 = jnp.tile(xp, (1, 1, 4))
            kk = kk * cmk4 + xp4 * (1.0 - cmk4)
            rr = jax.nn.sigmoid(xn * cmr + xp * (1.0 - cmr))
            vv = jnp.square(jax.nn.relu(kk)) @ W_cp
            x = x + rr * vv
            return (x, new_state)
        return _reference_tuple_inner(x, time_decay, time_first, W_tm, g1, b1, tmk, tmv, tmr, W_cm, W_cp, g2, b2, cmk, cmr)[0]

    def _L0_ffn_ref(x, in_proj_w, in_proj_b, out_w, out_b, ln1_g, ln1_b, router_w, router_b, w1, b1, w2, b2, ln2_g, ln2_b):
        import jax, jax.numpy as jnp
        import numpy as np
        H = 16
        E = 8
        EPS = 1e-05

        def _layernorm(x, g, b):
            mu = jnp.mean(x, axis=-1, keepdims=True)
            var = jnp.mean(jnp.square(x - mu), axis=-1, keepdims=True)
            return (x - mu) * jax.lax.rsqrt(var + EPS) * g + b
        T, B, C = x.shape
        D = C // H
        qkv = x @ in_proj_w.T + in_proj_b
        q, k, v = jnp.split(qkv, 3, axis=-1)
        q = q.reshape(T, B, H, D)
        k = k.reshape(T, B, H, D)
        v = v.reshape(T, B, H, D)
        scale = 1.0 / np.sqrt(D).astype(np.float32)
        scores = jnp.einsum('tbhd,sbhd->bhts', q, k) * scale
        attn = jax.nn.softmax(scores, axis=-1)
        ctx = jnp.einsum('bhts,sbhd->tbhd', attn, v).reshape(T, B, C)
        attn_out = ctx @ out_w.T + out_b
        h = _layernorm(x + attn_out, ln1_g, ln1_b)
        flat = h.reshape(-1, C)
        logits = flat @ router_w.T + router_b
        probs = jax.nn.softmax(logits, axis=-1)
        _, top_i = jax.lax.top_k(probs, 2)
        assign = jnp.max(top_i, axis=-1)
        out = jnp.zeros_like(flat)
        for e in range(E):
            he = jax.nn.gelu(flat @ w1[e].T + b1[e], approximate=False)
            oe = he @ w2[e].T + b2[e]
            out = jnp.where((assign == e)[:, None], oe, out)
        moe_out = out.reshape(T, B, C)
        return _layernorm(h + moe_out, ln2_g, ln2_b)
    x = L0_attn_x
    x = x + _L0_attn_ref(_layernorm(x, axis=-1), L0_attn_time_decay, L0_attn_time_first, L0_attn_W_tm, L0_attn_g1, L0_attn_b1, L0_attn_tmk, L0_attn_tmv, L0_attn_tmr, L0_attn_W_cm, L0_attn_W_cp, L0_attn_g2, L0_attn_b2, L0_attn_cmk, L0_attn_cmr)
    x = x + _L0_ffn_ref(_layernorm(x, axis=-1), L0_ffn_in_proj_w, L0_ffn_in_proj_b, L0_ffn_out_w, L0_ffn_out_b, L0_ffn_ln1_g, L0_ffn_ln1_b, L0_ffn_router_w, L0_ffn_router_b, L0_ffn_w1, L0_ffn_b1, L0_ffn_w2, L0_ffn_b2, L0_ffn_ln2_g, L0_ffn_ln2_b)
    return x

_drawn_inputs = setup_inputs


def setup_inputs(seed=0):
    import zlib

    import numpy as np

    out = dict(_drawn_inputs(seed))
    spreads = {'L0_attn_g1': (1.0, 0.2),
     'L0_attn_b1': (0.0, 0.1),
     'L0_attn_g2': (1.0, 0.6),
     'L0_attn_b2': (0.0, 0.392),
     'L0_ffn_in_proj_b': (0.0, 0.8),
     'L0_ffn_out_b': (0.0, 0.48),
     'L0_ffn_ln1_g': (1.0, 0.2),
     'L0_ffn_ln1_b': (0.0, 0.406),
     'L0_ffn_router_b': (0.0, 0.489),
     'L0_ffn_b1': (0.0, 0.8),
     'L0_ffn_b2': (0.0, 1.306),
     'L0_ffn_ln2_g': (1.0, 0.2),
     'L0_ffn_ln2_b': (0.0, 0.478)}
    factors = {'L0_attn_W_cm': 3.634,
     'L0_ffn_in_proj_w': 7.853,
     'L0_ffn_out_w': 6.327,
     'L0_ffn_router_w': 3.277,
     'L0_ffn_w1': 8.0,
     'L0_ffn_w2': 8.0}
    for name, (base, spread) in spreads.items():
        noise = np.random.default_rng([zlib.crc32(name.encode()), seed]).standard_normal(out[name].shape)
        drawn = base * np.exp(spread * noise) if base else spread * noise
        out[name] = jnp.asarray(drawn.astype(out[name].dtype))
    for name, factor in factors.items():
        out[name] = (out[name] * factor).astype(out[name].dtype)
    return out
```

```python
from contextlib import ExitStack

import concourse.bass as bass
from concourse import mybir

ALU = mybir.AluOpType
ACT = mybir.ActivationFunctionType
F32 = mybir.dt.float32
BF16 = mybir.dt.bfloat16
U32 = mybir.dt.uint32
X = mybir.AxisListType.X

B, T, C = 8, 512, 128
TC = 64
NCH = T // TC
N = B * TC
TILES = N // 128
E = 8
H, D = 16, 8
FF = 4
EPS = 1e-5
NEG_INF = -1e38
MASKED = -3e38
EXP_IS_ZERO = -104.0
ATT_SCALE = float(D) ** -0.5

CM, AT, EX = 2, 3, 4
SLOTS = NCH + EX

VEC = ["w", "u", "g1", "b1", "tmk", "tmv", "tmr", "g2", "b2", "cmk", "cmr", "bq", "bk", "bv", "bo",
       "g3", "b3", "g4", "b4"] + [f"be{e}" for e in range(E)]
VI = {name: i for i, name in enumerate(VEC)}
K_ID, K_CENTRE, K_MEAN, K_HEADS = 0, 128, 256, 384
K_IOTA = K_HEADS + H
K_EXPAND = K_IOTA + TILES * E
K_ALL = K_EXPAND + B * 128
W_TM, W_CM, W_CP = 0, 3 * C, 3 * C + FF * C
W_QKV = W_CP + FF * C
W_OUT = W_QKV + 3 * C
W_ROUTER = W_OUT + C
W_1 = W_ROUTER + E
W_2 = W_1 + E * C
W_ALL = W_2 + E * C
R_TM, R_CM, R_RB = 0, 3 * C, 4 * C
R_ALL = 4 * C + E


def build(nc, x, weights, vectors, rows, b2_experts, consts, penalty_rows, out):
    with ExitStack() as ctx:
        def sb(name, shape, dt=F32):
            return ctx.enter_context(nc.sbuf_tensor(name, shape, dt))

        def bank(name):
            return ctx.enter_context(nc.psum_tensor(name, [128, N], F32))

        def sem(name):
            return ctx.enter_context(nc.semaphore(name))

        wt = sb("wt", [128, W_ALL])
        vec = sb("vec", [128, len(VEC)])
        row = sb("row", [128, R_ALL])
        b2e = sb("b2e", [E, C])
        cst = sb("cst", [128, K_ALL])
        pen = sb("pen", [E, E * C], BF16)
        wrow = sb("wrow", [128, B, TC + 1])
        om = sb("om", [128, 5])
        half_u = sb("half_u", [128, 1])
        zero = sb("zero", [128, N])
        eps_c = sb("eps_c", [128, 1])
        ident = cst[:, K_ID:K_ID + 128]
        centre = cst[:, K_CENTRE:K_CENTRE + 128]
        mean = cst[:, K_MEAN:K_MEAN + 128]

        def V(name):
            return vec[:, VI[name]:VI[name] + 1]

        xres = sb("xres", [128, B, T])
        xl = sb("xl", [128, B, T + 1])
        x2 = sb("x2", [128, B, T + 1])

        xtok = sb("xtok", [128, TILES, C])
        stats = sb("stats", [128, TILES, 6])
        mv = sb("mv", [128, TILES, 2])
        ln_v = sb("ln_v", [128, TILES])
        inv_v = sb("inv_v", [128, TILES])
        r1 = sb("r1", [128, TILES])
        q2 = sb("q2", [128, TILES])
        ln_q = sb("ln_q", [128, TILES])
        ln_vq = sb("ln_vq", [128, TILES])
        r12 = sb("r12", [128, TILES])
        xltok = sb("xltok", [128, TILES, C])
        ztok = sb("ztok", [128, TILES, C])
        z = sb("z", [128, N])
        vv = sb("vv", [128, B, TC])
        rr = sb("rr", [128, B, TC])
        kx = sb("kx", [128, B, TC + 1])
        mx = sb("mx", [128, B, TC + 1])
        am = sb("am", [128, B, TC])
        bm = sb("bm", [128, B, TC])
        ax = sb("ax", [128, B, TC + 1])
        bx = sb("bx", [128, B, TC + 1])
        dx = sb("dx", [128, B, TC + 1])
        bbx = sb("bbx", [128, B, TC + 1])
        dl = sb("dl", [128, B, TC])
        t1 = sb("t1", [128, N])
        t2 = sb("t2", [128, N])
        alx = sb("alx", [128, B, TC + 1])
        bvx = sb("bvx", [128, B, TC + 1])
        aax = sb("aax", [128, B, TC + 1])
        df = sb("df", [128, B, TC])
        ty = sb("ty", [128, B, TC])

        sqr = {s: sb("sqr_" + s, [128, N]) for s in "cahe"}
        rstd = {s: sb("rstd_" + s, [128, N]) for s in "cahe"}

        xn = sb("xn", [128, N])
        xpk = sb("xpk", [128, B, TC])
        xpr = sb("xpr", [128, B, TC])
        kk = sb("kk", [128, 2, N])
        kk2 = sb("kk2", [128, FF, N])
        xs = sb("xs", [128, B, TC])

        x3 = sb("x3", [128, N])
        qkv = sb("qkv", [128, 3, N])
        prod = sb("prod", [128, B, N])
        sm = sb("sm", [128, TILES, B, H])
        pr = sb("pr", [128, TILES, B, H])
        smax = sb("smax", [128, TILES, H])
        ssum = sb("ssum", [128, TILES, H])
        sinv = sb("sinv", [128, TILES, H])
        attn = sb("attn", [128, N])
        y4 = sb("y4", [128, N])
        h = sb("h", [128, N])
        lg = sb("lg", [128, TILES, E])
        lmax = sb("lmax", [128, TILES])
        top = sb("top", [128, TILES, 8])
        topi = sb("topi", [128, TILES, 8], U32)
        assign = sb("assign", [128, TILES])
        mask = sb("mask", [128, TILES, E])
        maskt = sb("maskt", [E, N])
        unmask = sb("unmask", [E, N], BF16)

        he = sb("he", [128, 2, N])
        f5 = sb("f5", [128, N])
        fo = sb("fo", [128, B, TC])
        otok = sb("otok", [128, TILES, C])

        pA, pB, pC = [bank("pA0"), bank("pA1")], [bank("pB0"), bank("pB1")], [bank("pC0"), bank("pC1")]
        pAcc, pMoe = bank("pAcc"), bank("pMoe")

        s_params = sem("s_params")
        s_const = sem("s_const")
        s_pool0 = sem("s_pool0")
        s_passed_dve, s_passed_pool = sem("s_passed_dve"), sem("s_passed_pool")
        s_x = sem("s_x")
        s_stats, s_mv, s_r1, s_q2, s_lnq, s_lnvq, s_r12 = (
            sem(n) for n in ("s_stats", "s_mv", "s_r1", "s_q2", "s_lnq", "s_lnvq", "s_r12"))
        s_norm = sem("s_norm")
        s_xT, s_xlT, s_zT = sem("s_xT"), sem("s_xlT"), sem("s_zT")
        s_xTe, s_xlTe, s_zTe = sem("s_xTe"), sem("s_xlTe"), sem("s_zTe")
        s_prev0 = sem("s_prev0")
        s_kps, s_vps, s_rps = sem("s_kps"), sem("s_vps"), sem("s_rps")
        s_k, s_v, s_r = sem("s_k"), sem("s_v"), sem("s_r")
        s_m, s_kcarry = sem("s_m"), sem("s_kcarry")
        s_am, s_bm, s_ab = sem("s_am"), sem("s_bm"), sem("s_ab")
        s_d, s_dcarry, s_lnd = sem("s_d"), sem("s_dcarry"), sem("s_lnd")
        s_bb, s_dl, s_t12, s_alpha = sem("s_bb"), sem("s_dl"), sem("s_t12"), sem("s_alpha")
        s_bv, s_aa, s_aacarry, s_df = sem("s_bv"), sem("s_aa"), sem("s_aacarry"), sem("s_df")
        s_th, s_ysteps, s_x2 = sem("s_th"), sem("s_ysteps"), sem("s_x2")
        s_wrap = sem("s_wrap")
        s_cen = {s: sem("s_cen_" + s) for s in "cahe"}
        s_sq = {s: sem("s_sq_" + s) for s in "cahe"}
        s_var = {s: sem("s_var_" + s) for s in "cahe"}
        s_lnr = {s: sem("s_lnr_" + s) for s in "cahe"}
        s_rstd = {s: sem("s_rstd_" + s) for s in "cahe"}
        s_nrm = {s: sem("s_nrm_" + s) for s in "cahe"}
        s_xn, s_xp = sem("s_xn"), sem("s_xp")
        s_kk, s_kkm, s_kk2 = sem("s_kk"), sem("s_kkm"), sem("s_kk2")
        s_vvps, s_tr, s_thc, s_o1, s_xs, s_xres = (
            sem(n) for n in ("s_vvps", "s_tr", "s_thc", "s_o1", "s_xs", "s_xres"))
        s_qkvps, s_qkv = sem("s_qkvps"), sem("s_qkv")
        s_prod, s_score = sem("s_prod"), sem("s_score")
        s_smax, s_sm, s_pr, s_ssum, s_sinv, s_a = (
            sem(n) for n in ("s_smax", "s_sm", "s_pr", "s_ssum", "s_sinv", "s_a"))
        s_aT, s_attn = sem("s_aT"), sem("s_attn")
        s_exp, s_pv = sem("s_exp"), sem("s_pv")
        s_add, s_ops, s_y4 = sem("s_add"), sem("s_ops"), sem("s_y4")
        s_h, s_lgps, s_lg, s_top = sem("s_h"), sem("s_lgps"), sem("s_lg"), sem("s_top")
        s_lgsteps = sem("s_lgsteps")
        s_assign, s_mask, s_maskps, s_maskt = (
            sem(n) for n in ("s_assign", "s_mask", "s_maskps", "s_maskt"))
        s_pre, s_he, s_moe = sem("s_pre"), sem("s_he"), sem("s_moe")
        s_f5, s_fa, s_fo, s_oT, s_otok = sem("s_f5"), sem("s_fa"), sem("s_fo"), sem("s_oT"), sem("s_otok")
        s_out = sem("s_out")

        def v3(ap):
            return ap.rearrange("p (b t) -> p b t", b=B)

        def cols(first, j):
            if isinstance(j, int):
                return slice(first + (j + 1) % NCH * TC, first + (j + 1) % NCH * TC + TC)
            return bass.ds(j * TC + (first + TC), TC)

        def cols_tm(first, n):
            if isinstance(n, int):
                return slice(first + n * TC, first + n * TC + TC)
            return bass.ds(n * TC + first, TC)

        def after(eng, s, count):
            if not isinstance(count, int) or count > 0:
                eng.wait_ge(s, count)

        def own_wait(eng, passed):
            eng.sem_inc(passed, 1)

        def active(s, stage):
            return not isinstance(s, int) or stage <= s < stage + NCH

        def run_slots(eng, slot):
            for s in range(EX + 1):
                slot(s)
            with eng.Fori(EX + 1, NCH) as s:
                slot(s)
            for s in range(NCH, SLOTS):
                slot(s)

        LOADS = 7
        block = ctx.enter_context(nc.Block())

        @block.sync
        def _(sp):
            x_rows = x.rearrange("(j b) t c -> b t j c", b=2)
            o_rows = out.rearrange("(j b) t c -> b t j c", b=2)

            def load_x(n):
                after(sp, s_norm, n)
                after(sp, s_xT, n)
                for half in range(2):
                    sp.dma_start(xtok[TC * half:TC * half + TC, :, :],
                                 x_rows[half, cols_tm(0, n)]).then_inc(s_x, 16)

            def store(j):
                sp.wait_ge(s_otok, j + 1)
                for half in range(2):
                    sp.dma_start(o_rows[half, cols(0, j)],
                                 otok[TC * half:TC * half + TC, :, :]).then_inc(s_out, 16)

            load_x(0)
            sp.dma_start(cst[:, :], consts).then_inc(s_params, 16)
            sp.dma_start(vec[:, :], vectors).then_inc(s_params, 16)
            sp.dma_start(row[:, :], rows).then_inc(s_params, 16)
            sp.dma_start(wt[:, 0:W_QKV], weights[:, 0:W_QKV]).then_inc(s_params, 16)
            sp.dma_start(wt[:, W_QKV:W_ALL], weights[:, W_QKV:W_ALL]).then_inc(s_params, 16)
            sp.dma_start(b2e[:, :], b2_experts).then_inc(s_params, 16)
            sp.dma_start(pen[:, :], penalty_rows).then_inc(s_params, 16)

            def slot(s):
                if active(s, 0) and not (isinstance(s, int) and s == 0):
                    load_x(s)
                if active(s, EX):
                    store(s - EX)

            run_slots(sp, slot)
            sp.wait_ge(s_out, 32 * NCH)

        @block.gpsimd
        def _(pool):
            g = nc.gpsimd
            g.memset(kx[:, :, 0:1], NEG_INF)
            g.memset(ax[:, :, 0:1], 0.0)
            g.memset(bx[:, :, 0:1], 1.0)
            g.memset(alx[:, :, 0:1], 0.0)
            g.memset(bvx[:, :, 0:1], 0.0)
            g.memset(wrow[:, :, 0:1], NEG_INF)
            g.memset(eps_c[:, :], EPS).then_inc(s_pool0, 1)
            pool.wait_ge(s_params, 16 * LOADS)

            def tm_m(n):
                pool.wait_ge(s_m, n + 1)
                after(pool, s_ab, n)
                g.tensor_tensor(am[:, :, :], mx[:, :, 0:TC], mx[:, :, 1:TC + 1], ALU.subtract).then_inc(s_am, 1)
                g.tensor_tensor(bm[:, :, :], kx[:, :, 1:TC + 1], mx[:, :, 1:TC + 1], ALU.subtract).then_inc(s_bm, 1)
                g.tensor_copy(kx[:, :, 0:1], mx[:, :, TC:TC + 1]).then_inc(s_kcarry, 1)

            def tm_bb(n):
                pool.wait_ge(s_d, n + 1)
                own_wait(pool, s_passed_pool)
                g.tensor_copy(bx[:, :, 0:1], dx[:, :, TC:TC + 1]).then_inc(s_dcarry, 1)
                pool.wait_ge(s_lnd, n + 1)
                g.tensor_tensor(bbx[:, :, :], bbx[:, :, :], mx[:, :, :], ALU.add).then_inc(s_bb, 1)
                pool.wait_ge(s_bb, n + 1)
                after(pool, s_th, n)
                after(pool, s_t12, n)
                g.tensor_tensor(dl[:, :, :], bbx[:, :, 0:TC], kx[:, :, 1:TC + 1], ALU.subtract).then_inc(s_dl, 1)

            def tm_bv(n):
                pool.wait_ge(s_alpha, n + 1)
                pool.wait_ge(s_v, n + 1)
                g.tensor_tensor(bvx[:, :, 1:TC + 1], v3(t2[:, :]), vv[:, :, :], ALU.mult).then_inc(s_bv, 1)

            def tm_df(n):
                pool.wait_ge(s_aa, n + 1)
                after(pool, s_x2, n)
                g.tensor_tensor(df[:, :, :], aax[:, :, 0:TC], vv[:, :, :], ALU.subtract).then_inc(s_df, 1)
                g.tensor_copy(bvx[:, :, 0:1], aax[:, :, TC:TC + 1]).then_inc(s_aacarry, 1)

            def cm_xn(j):
                pool.wait_ge(s_nrm["c"], j + 1)
                own_wait(pool, s_passed_pool)
                g.tensor_scalar(xn[:, :], xn[:, :], V("g2"), V("b2"), ALU.mult, ALU.add).then_inc(s_xn, 1)

            def cm_xs(j):
                pool.wait_ge(s_x2, (j + 2) if not isinstance(j, int) else min(j + 2, NCH))
                after(pool, s_xres, j)
                g.tensor_tensor(xs[:, :, :], xres[:, :, cols(0, j)], x2[:, :, cols(1, j)], ALU.add).then_inc(s_xs, 1)

            def at_add(j, step):
                if step < 4:
                    pool.wait_ge(s_pv, 8 * j + 2 * step + 2)
                    a, b = prod[:, 2 * step, :], prod[:, 2 * step + 1, :]
                elif step == 4:
                    pool.wait_ge(s_add, 6 * j + 4)
                    p4 = prod[:, :, :].rearrange("p (u w) n -> p u w n", w=4)
                    a, b = p4[:, :, 0, :], p4[:, :, 2, :]
                else:
                    pool.wait_ge(s_add, 6 * j + 5)
                    a, b = prod[:, 0, :], prod[:, 4, :]
                g.tensor_tensor(a, a, b, ALU.add).then_inc(s_add, 1)

            def at_h(j):
                pool.wait_ge(s_nrm["h"], j + 1)
                after(pool, s_f5, j)
                own_wait(pool, s_passed_pool)
                g.tensor_scalar(h[:, :], y4[:, :], V("g3"), V("b3"), ALU.mult, ALU.add).then_inc(s_h, 1)

            def ex_out(j):
                pool.wait_ge(s_fa, j + 1)
                g.tensor_tensor(fo[:, :, :], fo[:, :, :], xres[:, :, cols(0, j)], ALU.add).then_inc(s_fo, 1)

            def slot(s):
                tm, cm, at, ex = (active(s, k) for k in (0, CM, AT, EX))
                if cm:
                    cm_xn(s - CM)
                    cm_xs(s - CM)
                if tm:
                    tm_m(s)
                    tm_bb(s)
                    tm_bv(s)
                    tm_df(s)
                if at:
                    for step in range(6):
                        at_add(s - AT, step)
                    
                if ex:
                    ex_out(s - EX)
                if at:
                    at_h(s - AT)

            run_slots(pool, slot)

        @block.scalar
        def _(act):
            a = nc.scalar
            act.wait_ge(s_params, 16 * LOADS)
            act.wait_ge(s_pool0, 1)
            act.wait_ge(s_const, 4)
            eps = eps_c[:, 0:1]
            a.preload_act_table_set("natural_log_exp_and_others")

            def tm_stats(n):
                act.wait_ge(s_mv, n + 1)
                a.activation(ln_v[:, :], mv[:, :, 1], ACT.Ln, bias=eps).then_inc(s_r1, 1)
                act.wait_ge(s_r1, 3 * n + 1)
                after(act, s_norm, n)
                a.activation(inv_v[:, :], ln_v[:, :], ACT.Exp, scale=-1.0).then_inc(s_r1, 1)
                a.activation(r1[:, :], ln_v[:, :], ACT.Exp, scale=-0.5).then_inc(s_r1, 1)
                act.wait_ge(s_q2, n + 1)
                a.activation(ln_q[:, :], q2[:, :], ACT.Ln, bias=eps).then_inc(s_lnq, 1)
                act.wait_ge(s_lnvq, n + 1)
                a.activation(r12[:, :], ln_vq[:, :], ACT.Exp, scale=-0.5).then_inc(s_r12, 1)

            def tm_evac(n):
                act.wait_ge(s_xT, n + 1)
                a.copy(xres[:, :, cols_tm(0, n)], v3(pA[0][:, :])).then_inc(s_xTe, 1)
                act.wait_ge(s_xlT, n + 1)
                a.copy(xl[:, :, cols_tm(1, n)], v3(pA[1][:, :])).then_inc(s_xlTe, 1)
                if isinstance(n, int) and n == 0:
                    a.copy(xl[:, :, 0:1], v3(pA[1][:, :])[:, :, 0:1]).then_inc(s_prev0, 1)
                act.wait_ge(s_zT, n + 1)
                after(act, s_rps, n)
                a.activation(z[:, :], pA[0][:, :], ACT.Identity, scale=V("g1"), bias=V("b1")).then_inc(s_zTe, 1)

            def tm_ab(n):
                act.wait_ge(s_am, n + 1)
                after(act, s_d, n)
                a.activation(ax[:, :, 1:TC + 1], am[:, :, :], ACT.Exp, bias=V("w"))
                act.wait_ge(s_bm, n + 1)
                a.activation(bx[:, :, 1:TC + 1], bm[:, :, :], ACT.Exp).then_inc(s_ab, 1)

            def tm_lnd(n):
                act.wait_ge(s_d, n + 1)
                after(act, s_dl, n)
                a.activation(bbx[:, :, :], dx[:, :, :], ACT.Ln).then_inc(s_lnd, 1)

            def tm_alpha(n):
                act.wait_ge(s_t12, n + 1)
                after(act, s_aa, n)
                a.activation(alx[:, :, 1:TC + 1], v3(t1[:, :]), ACT.Exp)
                a.activation(t2[:, :], t2[:, :], ACT.Exp, scale=-1.0).then_inc(s_alpha, 1)

            def tm_tanh(n):
                act.wait_ge(s_t12, n + 1)
                act.wait_ge(s_dl, n + 1)
                a.activation(dl[:, :, :], dl[:, :, :], ACT.Tanh, scale=0.5, bias=half_u[:, 0:1])
                act.wait_ge(s_r, n + 1)
                a.activation(rr[:, :, :], rr[:, :, :], ACT.Tanh, scale=0.5).then_inc(s_th, 1)

            def ln_square(st, cen, j):
                act.wait_ge(s_cen[st], j + 1)
                after(act, s_var[st], j)
                a.activation(sqr[st][:, :], cen[:, :], ACT.Square).then_inc(s_sq[st], 1)

            def ln_rstd(st, var, j):
                act.wait_ge(s_var[st], j + 1)
                after(act, s_nrm[st], j)
                a.activation(rstd[st][:, :], var[:, :], ACT.Ln, bias=eps).then_inc(s_lnr[st], 1)
                act.wait_ge(s_lnr[st], j + 1)
                a.activation(rstd[st][:, :], rstd[st][:, :], ACT.Exp, scale=-0.5).then_inc(s_rstd[st], 1)

            def cm_tanh(j):
                act.wait_ge(s_tr, j + 1)
                a.activation(xpr[:, :, :], xpr[:, :, :], ACT.Tanh, scale=0.5).then_inc(s_thc, 1)

            def at_qkv(j, i):
                act.wait_ge(s_qkvps, 3 * j + i + 1)
                if i < 2:
                    after(act, s_prod, 4 * j)
                else:
                    after(act, s_pv, 8 * j)
                a.activation(qkv[:, i, :], pB[i % 2][:, :] if i else pB[0][:, :], ACT.Identity,
                             bias=V(("bq", "bk", "bv")[i])).then_inc(s_qkv, 1)

            def at_exp(j):
                act.wait_ge(s_sm, j + 1)
                after(act, s_aT, j)
                a.activation(pr[:, :, :, :], sm[:, :, :, :], ACT.Exp, scale=ATT_SCALE).then_inc(s_pr, 1)

            def at_attn(j):
                act.wait_ge(s_aT, j + 1)
                after(act, s_exp, 8 * j)
                a.copy(attn[:, :], pB[0][:, :]).then_inc(s_attn, 1)

            def at_mask(j):
                act.wait_ge(s_maskps, j + 1)
                after(act, s_moe, 8 * j)
                a.copy(maskt[:, :], pB[0][0:E, :])
                a.activation(unmask[:, :], pB[0][0:E, :], ACT.Identity, scale=-1.0,
                             bias=1.0).then_inc(s_maskt, 1)

            def ex_gelu(j, e):
                act.wait_ge(s_pre, 8 * j + e + 1)
                after(act, s_moe, 8 * j + e - 1)
                a.activation(he[:, e % 2, :], pC[e % 2][:, :], ACT.Gelu, bias=V(f"be{e}")).then_inc(s_he, 1)

            def ex_affine(j):
                act.wait_ge(s_nrm["e"], j + 1)
                after(act, s_oT, j)
                a.activation(fo[:, :, :], v3(f5[:, :]), ACT.Identity, scale=V("g4"), bias=V("b4")).then_inc(s_fa, 1)

            def ex_store(j):
                act.wait_ge(s_oT, j + 1)
                after(act, s_out, 32 * j)
                a.copy(otok[:, :, :], pC[0][:, :].rearrange("p (j c) -> p j c", c=C)).then_inc(s_otok, 1)

            def slot(s):
                tm, cm, at, ex = (active(s, k) for k in (0, CM, AT, EX))
                if at:
                    ln_square("a", pB[0], s - AT)
                if cm:
                    ln_square("c", pA[0], s - CM)
                if tm:
                    tm_stats(s)
                if at:
                    ln_rstd("a", pB[1], s - AT)
                if cm:
                    ln_rstd("c", pA[1], s - CM)
                if at:
                    for i in range(3):
                        at_qkv(s - AT, i)
                if tm:
                    tm_evac(s)
                    tm_ab(s)
                    tm_lnd(s)
                if at:
                    at_exp(s - AT)
                if tm:
                    tm_alpha(s)
                if at:
                    at_attn(s - AT)
                a.preload_act_table_set("gelu_and_others")
                if tm:
                    tm_tanh(s)
                if cm:
                    cm_tanh(s - CM)
                if ex:
                    for e in range(E):
                        ex_gelu(s - EX, e)
                a.preload_act_table_set("natural_log_exp_and_others")
                if ex:
                    ln_square("e", pC[0], s - EX)
                    ln_rstd("e", pC[1], s - EX)
                if at:
                    ln_square("h", pB[1], s - AT)
                    ln_rstd("h", pB[0], s - AT)
                if ex:
                    ex_affine(s - EX)
                if at:
                    at_mask(s - AT)
                if ex:
                    ex_store(s - EX)

            run_slots(act, slot)

        @block.vector
        def _(dve):
            v = nc.vector
            dve.wait_ge(s_params, 16 * LOADS)
            dve.wait_ge(s_pool0, 1)
            v.tensor_scalar(om[:, 0:3], vec[:, VI["tmk"]:VI["tmk"] + 3], -1.0, 1.0, ALU.mult, ALU.add)
            v.tensor_scalar(om[:, 3:5], vec[:, VI["cmk"]:VI["cmk"] + 2], -1.0, 1.0, ALU.mult, ALU.add)
            v.tensor_scalar(half_u[:, :], V("u"), -0.5, None, ALU.mult).then_inc(s_const, 1)
            v.memset(zero[:, :], 0.0).then_inc(s_const, 1)
            v.tensor_tensor(wt[:, W_TM:W_TM + 3 * C], wt[:, W_TM:W_TM + 3 * C], row[:, R_TM:R_TM + 3 * C],
                            ALU.mult).then_inc(s_const, 1)
            v.tensor_tensor(wt[:, W_CM:W_CM + FF * C].rearrange("p (f c) -> p f c", f=FF),
                            wt[:, W_CM:W_CM + FF * C].rearrange("p (f c) -> p f c", f=FF),
                            row[:, R_CM:R_CM + C].unsqueeze(1).broadcast_to([128, FF, C]),
                            ALU.mult).then_inc(s_const, 1)
            dve.wait_ge(s_const, 4)
            v.tensor_scalar(wrow[:, :, 1:TC + 1], v3(zero[:, :]), V("w"), None, ALU.add).then_inc(s_const, 1)
            dve.wait_ge(s_const, 5)

            def tm_stats(n):
                dve.wait_ge(s_x, 32 * n + 32)
                for i in range(TILES):
                    ins = v.bn_stats(stats[:, i, :], xtok[:, i, :])
                ins.then_inc(s_stats, 1)
                dve.wait_ge(s_stats, n + 1)
                own_wait(dve, s_passed_dve)
                for i in range(TILES):
                    ins = v.bn_aggr(mv[:, i, :], stats[:, i, :])
                ins.then_inc(s_mv, 1)

            def tm_q2(n):
                dve.wait_ge(s_r1, 3 * n + 2)
                v.tensor_tensor(q2[:, :], mv[:, :, 1], inv_v[:, :], ALU.mult).then_inc(s_q2, 1)
                dve.wait_ge(s_lnq, n + 1)
                v.tensor_tensor(ln_vq[:, :], ln_v[:, :], ln_q[:, :], ALU.add).then_inc(s_lnvq, 1)

            def tm_norm(n):
                dve.wait_ge(s_r1, 3 * n + 3)
                dve.wait_ge(s_r12, n + 1)
                after(dve, s_zT, n)
                for i in range(TILES):
                    v.tensor_scalar(xltok[:, i, :], xtok[:, i, :], mv[:, i, 0:1], r1[:, i:i + 1],
                                    ALU.subtract, ALU.mult)
                    ins = v.tensor_scalar(ztok[:, i, :], xtok[:, i, :], mv[:, i, 0:1], r12[:, i:i + 1],
                                          ALU.subtract, ALU.mult)
                ins.then_inc(s_norm, 1)

            def tm_kvr(n):
                prev = xl[:, :, cols_tm(0, n)]
                dve.wait_ge(s_xlTe, n + 1)
                dve.wait_ge(s_prev0, 1)
                dve.wait_ge(s_kps, n + 1)
                after(dve, s_dl, n)
                v.scalar_tensor_tensor(kx[:, :, 1:TC + 1], prev, om[:, 0:1], v3(pA[1][:, :]),
                                       ALU.mult, ALU.add).then_inc(s_k, 1)
                dve.wait_ge(s_vps, n + 1)
                v.scalar_tensor_tensor(vv[:, :, :], prev, om[:, 1:2], v3(pA[0][:, :]),
                                       ALU.mult, ALU.add).then_inc(s_v, 1)
                dve.wait_ge(s_k, n + 1)
                after(dve, s_kcarry, n)
                after(dve, s_bb, n)
                v.tensor_tensor_scan(mx[:, :, :].rearrange("p b t -> p (b t)"),
                                     wrow[:, :, :].rearrange("p b t -> p (b t)"),
                                     kx[:, :, :].rearrange("p b t -> p (b t)"), NEG_INF,
                                     ALU.add, ALU.max).then_inc(s_m, 1)
                dve.wait_ge(s_rps, n + 1)
                v.scalar_tensor_tensor(rr[:, :, :], prev, om[:, 2:3], v3(pA[1][:, :]),
                                       ALU.mult, ALU.add).then_inc(s_r, 1)

            def tm_d(n):
                dve.wait_ge(s_ab, n + 1)
                after(dve, s_dcarry, n)
                after(dve, s_lnd, n)
                v.tensor_tensor_scan(dx[:, :, :].rearrange("p b t -> p (b t)"),
                                     ax[:, :, :].rearrange("p b t -> p (b t)"),
                                     bx[:, :, :].rearrange("p b t -> p (b t)"), 0.0,
                                     ALU.mult, ALU.add).then_inc(s_d, 1)

            def tm_t12(n):
                dve.wait_ge(s_dl, n + 1)
                after(dve, s_bv, n)
                v.tensor_scalar(v3(t1[:, :]), dl[:, :, :], V("w"), 0.0, ALU.add, ALU.min)
                v.tensor_scalar(v3(t2[:, :]), dl[:, :, :], V("w"), 0.0, ALU.add, ALU.max).then_inc(s_t12, 1)

            def tm_aa(n):
                dve.wait_ge(s_bv, n + 1)
                after(dve, s_aacarry, n)
                v.tensor_tensor_scan(aax[:, :, :].rearrange("p b t -> p (b t)"),
                                     alx[:, :, :].rearrange("p b t -> p (b t)"),
                                     bvx[:, :, :].rearrange("p b t -> p (b t)"), 0.0,
                                     ALU.mult, ALU.add).then_inc(s_aa, 1)

            def tm_y(n):
                dve.wait_ge(s_df, n + 1)
                dve.wait_ge(s_th, n + 1)
                v.scalar_tensor_tensor(ty[:, :, :], dl[:, :, :], 1.0, df[:, :, :],
                                       ALU.add, ALU.mult).then_inc(s_ysteps, 1)
                dve.wait_ge(s_ysteps, 3 * n + 1)
                v.scalar_tensor_tensor(ty[:, :, :], vv[:, :, :], 2.0, ty[:, :, :],
                                       ALU.mult, ALU.add).then_inc(s_ysteps, 1)
                dve.wait_ge(s_ysteps, 3 * n + 2)
                v.scalar_tensor_tensor(ty[:, :, :], rr[:, :, :], 1.0, ty[:, :, :],
                                       ALU.add, ALU.mult).then_inc(s_ysteps, 1)
                dve.wait_ge(s_ysteps, 3 * n + 3)
                v.scalar_tensor_tensor(x2[:, :, cols_tm(1, n)], ty[:, :, :], 0.25, xl[:, :, cols_tm(1, n)],
                                       ALU.mult, ALU.add).then_inc(s_x2, 1)

            def tm_wrap():
                dve.wait_ge(s_x2, NCH)
                v.tensor_copy(x2[:, :, 0:1], x2[:, :, T:T + 1]).then_inc(s_wrap, 1)

            def ln_scale(st, cen, dst, j):
                dve.wait_ge(s_rstd[st], j + 1)
                v.tensor_tensor(dst[:, :], cen[:, :], rstd[st][:, :], ALU.mult).then_inc(s_nrm[st], 1)

            def cm_scale(j):
                after(dve, s_tr, j)
                after(dve, s_kk, 4 * j)
                ln_scale("c", pA[0], xn, j)

            def cm_prev(j):
                if isinstance(j, int) and j == NCH - 1:
                    dve.wait_ge(s_wrap, 1)
                prev = x2[:, :, cols(0, j)]
                after(dve, s_o1, j)
                after(dve, s_kkm, 4 * j)
                v.tensor_scalar(xpk[:, :, :], prev, om[:, 3:4], None, ALU.mult)
                v.tensor_scalar(xpr[:, :, :], prev, om[:, 4:5], None, ALU.mult).then_inc(s_xp, 1)

            def cm_gate(j):
                dve.wait_ge(s_xn, j + 1)
                dve.wait_ge(s_xp, j + 1)
                v.scalar_tensor_tensor(xpr[:, :, :], v3(xn[:, :]), V("cmr"), xpr[:, :, :],
                                       ALU.mult, ALU.add).then_inc(s_tr, 1)

            def cm_hidden(j, f):
                dve.wait_ge(s_kk, 4 * j + f + 1)
                dve.wait_ge(s_xp, j + 1)
                after(dve, s_kk2, 4 * j + f - 1)
                v.tensor_tensor(v3(kk[:, f % 2, :]), v3(pA[f % 2][:, :]), xpk[:, :, :], ALU.add).then_inc(s_kkm, 1)
                dve.wait_ge(s_kkm, 4 * j + f + 1)
                after(dve, s_vvps, j)
                v.scalar_tensor_tensor(kk2[:, f, :], kk[:, f % 2, :], 0.0, kk[:, f % 2, :],
                                       ALU.max, ALU.mult).then_inc(s_kk2, 1)

            def cm_out(j):
                dve.wait_ge(s_thc, j + 1)
                dve.wait_ge(s_vvps, j + 1)
                v.scalar_tensor_tensor(xpr[:, :, :], xpr[:, :, :], 1.0, v3(pAcc[:, :]),
                                       ALU.add, ALU.mult).then_inc(s_o1, 1)
                dve.wait_ge(s_o1, j + 1)
                dve.wait_ge(s_xs, j + 1)
                v.scalar_tensor_tensor(xres[:, :, cols(0, j)], xpr[:, :, :], 0.5, xs[:, :, :],
                                       ALU.mult, ALU.add).then_inc(s_xres, 1)

            def at_scale(j):
                after(dve, s_y4, j)
                ln_scale("a", pB[0], x3, j)

            def at_prod(j, i):
                dve.wait_ge(s_qkv, 3 * j + 2)
                after(dve, s_add, 6 * j)
                after(dve, s_ops, j)
                q = v3(qkv[:, 0, :]).unsqueeze(1).broadcast_to([128, 2, B, TC])
                k = v3(qkv[:, 1, :])[:, 2 * i:2 * i + 2, :].unsqueeze(2).broadcast_to([128, 2, B, TC])
                v.tensor_tensor(prod[:, 2 * i:2 * i + 2, :].rearrange("p s (b t) -> p s b t", b=B), q, k,
                                ALU.mult).then_inc(s_prod, 1)

            def at_softmax_in(j):
                dve.wait_ge(s_score, 4 * j + 4)
                S = pB[1][:, :].rearrange("p (j s h) -> p j s h", j=TILES, s=B)
                v.tensor_reduce(smax[:, :, :], S.rearrange("p j s h -> p j h s"), X, ALU.max).then_inc(s_smax, 1)
                dve.wait_ge(s_smax, j + 1)
                after(dve, s_pr, j)
                v.tensor_tensor(sm[:, :, :, :], S, smax[:, :, :].unsqueeze(2).broadcast_to([128, TILES, B, H]),
                                ALU.subtract).then_inc(s_sm, 1)

            def at_softmax_out(j):
                dve.wait_ge(s_pr, j + 1)
                v.tensor_reduce(ssum[:, :, :], pr[:, :, :, :].rearrange("p j s h -> p j h s"), X,
                                ALU.add).then_inc(s_ssum, 1)
                dve.wait_ge(s_ssum, j + 1)
                v.reciprocal(sinv[:, :, :], ssum[:, :, :]).then_inc(s_sinv, 1)
                dve.wait_ge(s_sinv, j + 1)
                v.tensor_tensor(pr[:, :, :, :], pr[:, :, :, :],
                                sinv[:, :, :].unsqueeze(2).broadcast_to([128, TILES, B, H]),
                                ALU.mult).then_inc(s_a, 1)

            def at_pv(j, s):
                dve.wait_ge(s_exp, 8 * j + s + 1)
                if s == 0:
                    dve.wait_ge(s_qkv, 3 * j + 3)
                val = v3(qkv[:, 2, :])[:, s:s + 1, :].broadcast_to([128, B, TC])
                v.tensor_tensor(v3(prod[:, s, :]), v3(pB[(s + 1) % 2][:, :]), val, ALU.mult).then_inc(s_pv, 1)

            def at_y(j):
                dve.wait_ge(s_ops, j + 1)
                after(dve, s_h, j)
                v.scalar_tensor_tensor(y4[:, :], pAcc[:, :], V("bo"), x3[:, :], ALU.add, ALU.add).then_inc(s_y4, 1)

            def at_h(j):
                dve.wait_ge(s_cen["h"], j + 1)
                ln_scale("h", pB[1], y4, j)

            def at_route(j):
                dve.wait_ge(s_lgps, j + 1)
                v.tensor_tensor(lg[:, :, :], pB[1][:, 0:TILES * E].rearrange("p (j e) -> p j e", e=E),
                                row[:, R_RB:R_RB + E].unsqueeze(1).broadcast_to([128, TILES, E]),
                                ALU.add).then_inc(s_lgsteps, 1)
                dve.wait_ge(s_lgsteps, 4 * j + 1)
                v.tensor_reduce(lmax[:, :], lg[:, :, :], X, ALU.max).then_inc(s_lgsteps, 1)
                dve.wait_ge(s_lgsteps, 4 * j + 2)
                v.tensor_tensor(lg[:, :, :], lg[:, :, :], lmax[:, :].unsqueeze(2).broadcast_to([128, TILES, E]),
                                ALU.subtract).then_inc(s_lgsteps, 1)
                dve.wait_ge(s_lgsteps, 4 * j + 3)
                v.tensor_scalar(lg[:, :, :], lg[:, :, :], EXP_IS_ZERO, None, ALU.max).then_inc(s_lgsteps, 1)
                dve.wait_ge(s_lgsteps, 4 * j + 4)
                own_wait(dve, s_passed_dve)
                for i in range(TILES):
                    ins = v.max(top[:, i, :], lg[:, i, :])
                ins.then_inc(s_top, 1)
                dve.wait_ge(s_top, 2 * j + 1)
                own_wait(dve, s_passed_dve)
                for i in range(TILES):
                    ins = v.max_index(topi[:, i, :], top[:, i, :], lg[:, i, :])
                ins.then_inc(s_top, 1)
                dve.wait_ge(s_top, 2 * j + 2)
                v.tensor_tensor(assign[:, :], topi[:, :, 0], topi[:, :, 1], ALU.max).then_inc(s_assign, 1)
                dve.wait_ge(s_assign, j + 1)
                after(dve, s_maskps, j)
                v.tensor_tensor(mask[:, :, :], cst[:, K_IOTA:K_IOTA + TILES * E].rearrange("p (j e) -> p j e", e=E),
                                assign[:, :].unsqueeze(2).broadcast_to([128, TILES, E]),
                                ALU.is_equal).then_inc(s_mask, 1)

            def ex_sum(j):
                dve.wait_ge(s_moe, 8 * j + 8)
                after(dve, s_fa, j)
                v.tensor_tensor(f5[:, :], pMoe[:, :], h[:, :], ALU.add).then_inc(s_f5, 1)

            def ex_scale(j):
                dve.wait_ge(s_cen["e"], j + 1)
                ln_scale("e", pC[0], f5, j)

            def slot(s):
                tm, cm, at, ex = (active(s, k) for k in (0, CM, AT, EX))
                if isinstance(s, int) and s == NCH:
                    tm_wrap()
                if tm:
                    tm_stats(s)
                    tm_q2(s)
                if at:
                    at_scale(s - AT)
                if tm:
                    tm_norm(s)
                if cm:
                    cm_scale(s - CM)
                    cm_prev(s - CM)
                if at:
                    at_prod(s - AT, 0)
                    at_prod(s - AT, 1)
                if tm:
                    tm_kvr(s)
                if at:
                    at_prod(s - AT, 2)
                    at_prod(s - AT, 3)
                if cm:
                    cm_gate(s - CM)
                if tm:
                    tm_d(s)
                if at:
                    at_softmax_in(s - AT)
                if tm:
                    tm_t12(s)
                if at:
                    at_softmax_out(s - AT)
                if cm:
                    for f in range(FF):
                        cm_hidden(s - CM, f)
                if tm:
                    tm_aa(s)
                if at:
                    at_pv(s - AT, 0)
                    at_pv(s - AT, 1)
                if tm:
                    tm_y(s)
                if at:
                    at_pv(s - AT, 2)
                    at_pv(s - AT, 3)
                if cm:
                    cm_out(s - CM)
                if at:
                    for i in range(4, 8):
                        at_pv(s - AT, i)
                    at_y(s - AT)
                if ex:
                    ex_sum(s - EX)
                    ex_scale(s - EX)
                if at:
                    at_h(s - AT)
                    at_route(s - AT)

            run_slots(dve, slot)

        @block.tensor
        def _(pe):
            t = nc.tensor
            pe.wait_ge(s_params, 16 * LOADS)
            pe.wait_ge(s_const, 4)

            def transposes(dst, src, done):
                for i in range(TILES):
                    ins = t.transpose(dst[:, 128 * i:128 * i + 128], src[:, i, :], ident)
                ins.then_inc(done, 1)

            def ln_centre(st, dst, src, j):
                t.matmul(dst, centre, src, start=True, stop=True).then_inc(s_cen[st], 1)

            def ln_var(st, dst, j):
                pe.wait_ge(s_sq[st], j + 1)
                t.matmul(dst[:, :], mean, sqr[st][:, :], start=True, stop=True).then_inc(s_var[st], 1)

            def tm_transpose(n, cm):
                pe.wait_ge(s_norm, n + 1)
                if cm:
                    pe.wait_ge(s_nrm["c"], n - CM + 1)
                else:
                    after(pe, s_v, n)
                transposes(pA[0], xtok, s_xT)
                if not cm:
                    after(pe, s_r, n)
                transposes(pA[1], xltok, s_xlT)
                pe.wait_ge(s_xTe, n + 1)
                transposes(pA[0], ztok, s_zT)

            def tm_kvr(n):
                pe.wait_ge(s_zTe, n + 1)
                pe.wait_ge(s_xlTe, n + 1)
                if isinstance(n, int) and n == 0:
                    pe.wait_ge(s_prev0, 1)
                t.matmul(pA[1][:, :], wt[:, W_TM:W_TM + C], z[:, :], start=True, stop=True).then_inc(s_kps, 1)
                t.matmul(pA[0][:, :], wt[:, W_TM + C:W_TM + 2 * C], z[:, :], start=True,
                         stop=True).then_inc(s_vps, 1)
                pe.wait_ge(s_k, n + 1)
                t.matmul(pA[1][:, :], wt[:, W_TM + 2 * C:W_TM + 3 * C], z[:, :], start=True,
                         stop=True).then_inc(s_rps, 1)

            def cm_centre(j):
                if isinstance(j, int) and j == 0:
                    pe.wait_ge(s_v, CM)
                    pe.wait_ge(s_r, CM)
                pe.wait_ge(s_x2, (j + 2) if not isinstance(j, int) else min(j + 2, NCH))
                after(pe, s_kkm, 4 * j)
                ln_centre("c", v3(pA[0][:, :]), x2[:, :, cols(1, j)], j)

            def cm_hidden(j, f, tm):
                if f == 0:
                    pe.wait_ge(s_xn, j + 1)
                    if tm:
                        pe.wait_ge(s_v, j + CM + 1)
                        pe.wait_ge(s_r, j + CM + 1)
                if f >= 2:
                    pe.wait_ge(s_kkm, 4 * j + f - 1)
                t.matmul(pA[f % 2][:, :], wt[:, W_CM + f * C:W_CM + f * C + C], xn[:, :], start=True,
                         stop=True).then_inc(s_kk, 1)

            def cm_mlp(j):
                after(pe, s_y4, j - 1)
                after(pe, s_o1, j)
                for f in range(FF):
                    pe.wait_ge(s_kk2, 4 * j + f + 1)
                    ins = t.matmul(pAcc[:, :], wt[:, W_CP + f * C:W_CP + f * C + C], kk2[:, f, :],
                                   start=(f == 0), stop=(f == FF - 1))
                ins.then_inc(s_vvps, 1)

            def at_centre(j):
                pe.wait_ge(s_xres, j + 1)
                after(pe, s_maskt, j)
                ln_centre("a", v3(pB[0][:, :]), xres[:, :, cols(0, j)], j)

            def at_qkv(j):
                pe.wait_ge(s_nrm["a"], j + 1)
                t.matmul(pB[0][:, :], wt[:, W_QKV:W_QKV + C], x3[:, :], start=True, stop=True).then_inc(s_qkvps, 1)
                t.matmul(pB[1][:, :], wt[:, W_QKV + C:W_QKV + 2 * C], x3[:, :], start=True,
                         stop=True).then_inc(s_qkvps, 1)
                pe.wait_ge(s_qkv, 3 * j + 1)
                t.matmul(pB[0][:, :], wt[:, W_QKV + 2 * C:W_QKV + 3 * C], x3[:, :], start=True,
                         stop=True).then_inc(s_qkvps, 1)

            def at_scores(j, i):
                pe.wait_ge(s_prod, 4 * j + i + 1)
                for s in (2 * i, 2 * i + 1):
                    for tile in range(TILES):
                        at = (tile * B + s) * H
                        ins = t.matmul(pB[1][:, at:at + H], prod[:, s, 128 * tile:128 * tile + 128],
                                       cst[:, K_HEADS:K_HEADS + H], start=True, stop=True)
                ins.then_inc(s_score, 1)

            def at_transpose(j):
                pe.wait_ge(s_a, j + 1)
                pe.wait_ge(s_qkv, 3 * j + 3)
                transposes(pB[0], pr[:, :, :, :].rearrange("p j s h -> p j (s h)"), s_aT)

            def at_expand(j, s):
                if s == 0:
                    pe.wait_ge(s_attn, j + 1)
                if s >= 2:
                    pe.wait_ge(s_pv, 8 * j + s - 1)
                t.matmul(pB[(s + 1) % 2][:, :], cst[:, K_EXPAND + s * 128:K_EXPAND + s * 128 + 128],
                         attn[:, :], start=True, stop=True).then_inc(s_exp, 1)

            def at_out(j, cm):
                pe.wait_ge(s_add, 6 * j + 6)
                if cm:
                    pe.wait_ge(s_o1, j + AT - CM + 1)
                t.matmul(pAcc[:, :], wt[:, W_OUT:W_OUT + C], prod[:, 0, :], start=True, stop=True).then_inc(s_ops, 1)

            def at_centre2(j):
                pe.wait_ge(s_y4, j + 1)
                ln_centre("h", pB[1][:, :], y4[:, :], j)

            def at_router(j):
                pe.wait_ge(s_h, j + 1)
                for i in range(TILES):
                    ins = t.matmul(pB[1][:, E * i:E * i + E], h[:, 128 * i:128 * i + 128],
                                   wt[:, W_ROUTER:W_ROUTER + E], start=True, stop=True)
                ins.then_inc(s_lgps, 1)

            def at_mask(j):
                pe.wait_ge(s_mask, j + 1)
                for i in range(TILES):
                    ins = t.transpose(pB[0][0:E, 128 * i:128 * i + 128], mask[:, i, :], ident)
                ins.then_inc(s_maskps, 1)

            def ex_in(j, e):
                if e == 0:
                    after(pe, s_otok, j)
                    pe.wait_ge(s_maskt, j + 1)
                if e >= 2:
                    pe.wait_ge(s_he, 8 * j + e - 1)
                t.matmul(pC[e % 2][:, :], wt[:, W_1 + e * C:W_1 + e * C + C], h[:, :], start=True, stop=False)
                t.matmul(pC[e % 2][:, :], pen[:, e * C:e * C + C], unmask[:, :], start=False,
                         stop=True).then_inc(s_pre, 1)

            def ex_out(j, e):
                pe.wait_ge(s_he, 8 * j + e + 1)
                if e == 0:
                    after(pe, s_f5, j)
                    t.matmul(pMoe[:, :], b2e[:, :], maskt[:, :], start=True, stop=False)
                t.matmul(pMoe[:, :], wt[:, W_2 + e * C:W_2 + e * C + C], he[:, e % 2, :], start=False,
                         stop=(e == E - 1)).then_inc(s_moe, 1)

            def ex_centre(j):
                pe.wait_ge(s_f5, j + 1)
                ln_centre("e", pC[0][:, :], f5[:, :], j)

            def ex_transpose(j):
                pe.wait_ge(s_fo, j + 1)
                transposes(pC[0], fo[:, :, :].rearrange("p (j b) t -> p j (b t)", b=2), s_oT)

            def slot(s):
                tm, cm, at, ex = (active(s, k) for k in (0, CM, AT, EX))
                if at:
                    at_centre(s - AT)
                if cm:
                    cm_centre(s - CM)
                if at:
                    ln_var("a", pB[1], s - AT)
                if cm:
                    ln_var("c", pA[1], s - CM)
                if at:
                    at_qkv(s - AT)
                if tm:
                    tm_transpose(s, cm)
                if at:
                    at_scores(s - AT, 0)
                    at_scores(s - AT, 1)
                if tm:
                    tm_kvr(s)
                if at:
                    at_scores(s - AT, 2)
                    at_scores(s - AT, 3)
                if cm:
                    for f in range(FF):
                        cm_hidden(s - CM, f, tm)
                if at:
                    at_transpose(s - AT)
                if cm:
                    cm_mlp(s - CM)
                for i in range(E):
                    if at:
                        at_expand(s - AT, i)
                    if ex:
                        ex_in(s - EX, i)
                        if i:
                            ex_out(s - EX, i - 1)
                if ex:
                    ex_out(s - EX, E - 1)
                if at:
                    at_out(s - AT, cm)
                if ex:
                    ex_centre(s - EX)
                    ln_var("e", pC[1], s - EX)
                if at:
                    at_centre2(s - AT)
                    ln_var("h", pB[0], s - AT)
                if ex:
                    ex_transpose(s - EX)
                if at:
                    at_router(s - AT)
                    at_mask(s - AT)

            run_slots(pe, slot)


def kernel(**inputs):
    import ml_dtypes
    import numpy as np
    import concourse.bacc as bacc
    from concourse.bass_utils import run_bass_kernel_spmd

    a = {k: np.asarray(v) for k, v in inputs.items()}
    A = {k[8:]: v for k, v in a.items() if k.startswith("L0_attn_")}
    Fm = {k[7:]: v for k, v in a.items() if k.startswith("L0_ffn_")}
    f = np.float32

    weights = np.concatenate([
        A["W_tm"], A["W_cm"],
        A["W_cp"].reshape(FF, C, C).transpose(1, 0, 2).reshape(C, FF * C),
        Fm["in_proj_w"].T, Fm["out_w"].T, Fm["router_w"].T,
        Fm["w1"].transpose(2, 0, 1).reshape(C, E * C),
        Fm["w2"].transpose(2, 0, 1).reshape(C, E * C)], axis=1)
    ib = Fm["in_proj_b"].reshape(3, C)
    cols = [A["time_decay"], A["time_first"], A["g1"], A["b1"], A["tmk"].reshape(C), A["tmv"].reshape(C),
            A["tmr"].reshape(C), A["g2"], A["b2"], A["cmk"].reshape(C), A["cmr"].reshape(C),
            ib[0], ib[1], ib[2], Fm["out_b"], Fm["ln1_g"], Fm["ln1_b"], Fm["ln2_g"], Fm["ln2_b"]]
    vectors = np.stack(cols + [Fm["b1"][e] for e in range(E)], axis=1)
    rows = np.concatenate([A["tmk"].reshape(C), A["tmv"].reshape(C), A["tmr"].reshape(C),
                           A["cmk"].reshape(C), Fm["router_b"]])
    rows = np.broadcast_to(rows[None, :], (128, R_ALL))

    eye = np.eye(128, dtype=f)
    average = np.full((128, 128), 1.0 / C, f)
    heads = np.repeat(np.eye(H, dtype=f), D, axis=0)
    iota = np.broadcast_to(np.tile(np.arange(E, dtype=f), TILES)[None, :], (128, TILES * E))
    expand = np.zeros((B, H, B, C), f)
    for s in range(B):
        expand[s, :, s, :] = heads.T
    consts = np.concatenate([eye, eye - average, average, heads, iota,
                             expand.reshape(B * H, B * C)], axis=1)
    penalty = np.zeros((E, E, C), ml_dtypes.bfloat16)
    for e in range(E):
        penalty[e, e, :] = MASKED
    host = {"x": a["L0_attn_x"], "weights": weights, "vectors": vectors, "rows": rows,
            "b2_experts": Fm["b2"], "consts": consts, "penalty_rows": penalty.reshape(E, E * C)}

    nc = bacc.Bacc("TRN2", target_bir_lowering=False, num_devices=1)
    arrays, args = {}, []
    for name, array in host.items():
        array = np.ascontiguousarray(array)
        arrays[name] = array
        args.append(nc.dram_tensor(name, array.shape, mybir.dt.from_np(array.dtype), kind="ExternalInput").ap())
    args.append(nc.dram_tensor("out", (B, T, C), F32, kind="ExternalOutput").ap())
    build(nc, *args)
    r = run_bass_kernel_spmd(nc, [arrays], core_ids=[0])
    return r.results[0]["out"]
```

```python
from contextlib import ExitStack

import concourse.bass as bass
from concourse import mybir

ALU = mybir.AluOpType
ACT = mybir.ActivationFunctionType
F32 = mybir.dt.float32
BF16 = mybir.dt.bfloat16
F32R = mybir.dt.float32r
U32 = mybir.dt.uint32
X = mybir.AxisListType.X

B, T, C = 8, 512, 128
TC = 64
NCH = T // TC
N = B * TC
TILES = N // 128
E = 8
H, D = 16, 8
FF = 4
EPS = 1e-5
NEG_INF = -1e38
MASKED = -3e38
EXP_IS_ZERO = -104.0
ATT_SCALE = float(D) ** -0.5

TM, CM, AT, EX = 0, 2, 3, 4
AHEAD = 2
LAST_LAG = 5
SLOTS = NCH + LAST_LAG

VEC = ["w", "u", "g1", "b1", "tmk", "tmv", "tmr", "g2", "b2", "cmk", "cmr", "bq", "bk", "bv", "bo",
       "g3", "b3", "g4", "b4"] + [f"be{e}" for e in range(E)]
VI = {name: i for i, name in enumerate(VEC)}
K_ID, K_CENTRE, K_MEAN, K_HEADS = 0, 128, 256, 384
K_IOTA = K_HEADS + 4 * H
K_RB = K_IOTA + TILES * E
K_ALL = K_RB + E
U_W1, U_SPREAD, U_ROWS, U_ZERO = 0, E * C, E * C + B * C, E * C + B * C + 4 * C
W_TM, W_CM, W_CP = 0, 3 * C, 3 * C + FF * C
W_QKV = W_CP + FF * C
W_OUT = W_QKV + 3 * C
W_ROUTER = W_OUT + C
W_2 = W_ROUTER + E
W_ALL = W_2 + E * C


def build(nc, x, weights, vectors, b2_experts, consts, setup_only, penalty_rows, out):
    with ExitStack() as ctx:
        def sb(name, shape, dt=F32):
            return ctx.enter_context(nc.sbuf_tensor(name, shape, dt))

        def bank(name):
            return ctx.enter_context(nc.psum_tensor(name, [128, N], F32))

        def sem(name):
            return ctx.enter_context(nc.semaphore(name))

        wt = sb("wt", [128, W_ALL])
        vec = sb("vec", [128, len(VEC)])
        b2e = sb("b2e", [E, C])
        cst = sb("cst", [128, K_ALL])
        pen = sb("pen", [E, E * C], BF16)
        wrow = sb("wrow", [128, B, TC + 1])
        om = sb("om", [128, 5])
        half_u = sb("half_u", [128, 1])
        eps_c = sb("eps_c", [128, 1])
        ident = cst[:, K_ID:K_ID + 128]
        centre = cst[:, K_CENTRE:K_CENTRE + 128]
        mean = cst[:, K_MEAN:K_MEAN + 128]

        router_bias = cst[:, K_RB:K_RB + E]

        def V(name):
            return vec[:, VI[name]:VI[name] + 1]

        xres = sb("xres", [128, B, T])
        xl = sb("xl", [128, B, T + 1])
        x2 = sb("x2", [128, B, T + 1])

        xtok = sb("xtok", [128, TILES, C])
        stats = sb("stats", [128, TILES, 6])
        mv = sb("mv", [128, TILES, 2])
        ln_v = sb("ln_v", [128, TILES])
        inv_v = sb("inv_v", [128, TILES])
        r1 = sb("r1", [128, TILES])
        q2 = sb("q2", [128, TILES])
        ln_q = sb("ln_q", [128, TILES])
        ln_vq = sb("ln_vq", [128, TILES])
        r12 = sb("r12", [128, TILES])
        xltok = sb("xltok", [128, TILES, C])
        ztok = sb("ztok", [128, TILES, C])
        z = sb("z", [128, N])
        vv = sb("vv", [128, B, TC])
        rr = sb("rr", [128, B, TC])
        kx = sb("kx", [128, B, TC + 1])
        mx = sb("mx", [128, B, TC + 1])
        ax = sb("ax", [128, B, TC + 1])
        bx = sb("bx", [128, B, TC + 1])
        dx = sb("dx", [128, B, TC + 1])
        bbx = sb("bbx", [128, B, TC + 1])
        dl = sb("dl", [128, B, TC])
        t1 = sb("t1", [128, N])
        t2 = sb("t2", [128, N])
        alx = sb("alx", [128, B, TC + 1])
        bvx = sb("bvx", [128, B, TC + 1])
        aax = sb("aax", [128, B, TC + 1])
        df = sb("df", [128, B, TC])
        ty = sb("ty", [128, B, TC])

        sqr = {s: sb("sqr_" + s, [128, N]) for s in "cahe"}
        rstd = sqr

        xn = sb("xn", [128, N])
        xpk = sb("xpk", [128, B, TC])
        xpr = sb("xpr", [128, B, TC])
        kk = sb("kk", [128, 2, N])
        kk2 = sb("kk2", [128, FF, N])
        xs = sb("xs", [128, B, TC])

        x3 = sb("x3", [128, N])
        qkv = sb("qkv", [128, 3, N])
        prod = sb("prod", [128, B, N])
        boot = prod[:, :, :].rearrange("p s n -> p (s n)")
        pr = sb("pr", [128, TILES, B, H])
        smax = sb("smax", [128, TILES, H])
        ssum = sb("ssum", [128, TILES, H])
        sinv = sb("sinv", [128, TILES, H])
        st = sb("st", [128, N])
        attn = sb("attn", [128, 2, N], F32R)
        spread = sb("spread", [128, B * C], F32R)
        y4 = sb("y4", [128, N])
        h = sb("h", [128, N])
        h2 = sb("h2", [128, 2, N], F32R)
        w1 = sb("w1", [128, 2, E * C], F32R)
        lg = sb("lg", [128, TILES, E])
        lmax = sb("lmax", [128, TILES])
        top = sb("top", [128, TILES, 8])
        topi = sb("topi", [128, TILES, 8], U32)
        assign = sb("assign", [128, TILES])
        mask = sb("mask", [128, TILES, E], BF16)
        ident16 = sb("ident16", [128, 128], BF16)
        maskt = sb("maskt", [E, N])
        unmask = sb("unmask", [E, N], BF16)

        he = sb("he", [128, 2, N])
        f5 = sb("f5", [128, N])
        fo = sb("fo", [128, B, TC])
        otok = sb("otok", [128, TILES, C])

        pA, pB, pC = [bank("pA0"), bank("pA1")], [bank("pB0"), bank("pB1")], [bank("pC0"), bank("pC1")]
        pAcc, pMoe = bank("pAcc"), bank("pMoe")

        s_params = sem("s_params")
        s_const = sem("s_const")
        s_pool0 = sem("s_pool0")
        s_passed_dve, s_passed_pool = sem("s_passed_dve"), sem("s_passed_pool")
        s_x = sem("s_x")
        s_stats, s_mv, s_r1, s_q2, s_lnq, s_lnvq, s_r12 = (
            sem(n) for n in ("s_stats", "s_mv", "s_r1", "s_q2", "s_lnq", "s_lnvq", "s_r12"))
        s_norm = sem("s_norm")
        s_xT, s_xlT, s_zT = sem("s_xT"), sem("s_xlT"), sem("s_zT")
        s_xTe, s_xlTe, s_zTe = sem("s_xTe"), sem("s_xlTe"), sem("s_zTe")
        s_prev0 = sem("s_prev0")
        s_kps, s_vps, s_rps = sem("s_kps"), sem("s_vps"), sem("s_rps")
        s_k, s_v, s_r = sem("s_k"), sem("s_v"), sem("s_r")
        s_m, s_kcarry = sem("s_m"), sem("s_kcarry")
        s_am, s_bm, s_ab = sem("s_am"), sem("s_bm"), sem("s_ab")
        s_d, s_dcarry, s_lnd = sem("s_d"), sem("s_dcarry"), sem("s_lnd")
        s_bb, s_dl, s_t12, s_alpha = sem("s_bb"), sem("s_dl"), sem("s_t12"), sem("s_alpha")
        s_bv, s_aa, s_aacarry, s_df = sem("s_bv"), sem("s_aa"), sem("s_aacarry"), sem("s_df")
        s_th, s_ysteps, s_x2 = sem("s_th"), sem("s_ysteps"), sem("s_x2")
        s_wrap = sem("s_wrap")
        s_cen = {s: sem("s_cen_" + s) for s in "cahe"}
        s_sq = {s: sem("s_sq_" + s) for s in "cahe"}
        s_var = {s: sem("s_var_" + s) for s in "cahe"}
        s_lnr = {s: sem("s_lnr_" + s) for s in "cahe"}
        s_rstd = {s: sem("s_rstd_" + s) for s in "cahe"}
        s_nrm = {s: sem("s_nrm_" + s) for s in "cahe"}
        s_xn, s_xp = sem("s_xn"), sem("s_xp")
        s_kk, s_kkm, s_kk2 = sem("s_kk"), sem("s_kkm"), sem("s_kk2")
        s_vvps, s_tr, s_thc, s_o1, s_xs, s_xres = (
            sem(n) for n in ("s_vvps", "s_tr", "s_thc", "s_o1", "s_xs", "s_xres"))
        s_qkvps, s_qkv = sem("s_qkvps"), sem("s_qkv")
        s_prod, s_score = sem("s_prod"), sem("s_score")
        s_st, s_sT, s_ahi = sem("s_st"), sem("s_sT"), sem("s_ahi")
        s_hhi, s_hlo = sem("s_hhi"), sem("s_hlo")
        s_smax, s_sm, s_pr, s_ssum, s_sinv, s_a = (
            sem(n) for n in ("s_smax", "s_sm", "s_pr", "s_ssum", "s_sinv", "s_a"))
        s_aT, s_attn = sem("s_aT"), sem("s_attn")
        s_exp, s_pv = sem("s_exp"), sem("s_pv")
        s_add, s_ops, s_y4 = sem("s_add"), sem("s_ops"), sem("s_y4")
        s_h, s_lgps, s_lg, s_top = sem("s_h"), sem("s_lgps"), sem("s_lg"), sem("s_top")
        s_lgsteps = sem("s_lgsteps")
        s_assign, s_mask, s_maskps, s_maskt = (
            sem(n) for n in ("s_assign", "s_mask", "s_maskps", "s_maskt"))
        s_pre, s_he, s_moe = sem("s_pre"), sem("s_he"), sem("s_moe")
        s_f5, s_fa, s_fo, s_oT, s_otok = sem("s_f5"), sem("s_fa"), sem("s_fo"), sem("s_oT"), sem("s_otok")
        s_out = sem("s_out")

        def v3(ap):
            return ap.rearrange("p (b t) -> p b t", b=B)

        def cols(first, j):
            if isinstance(j, int):
                return slice(first + (j + 1) % NCH * TC, first + (j + 1) % NCH * TC + TC)
            return bass.ds(j * TC + (first + TC), TC)

        def cols_tm(first, n):
            if isinstance(n, int):
                return slice(first + n * TC, first + n * TC + TC)
            return bass.ds(n * TC + first, TC)

        def after(eng, s, count):
            if not isinstance(count, int) or count > 0:
                eng.wait_ge(s, count)

        def own_wait(eng, passed):
            eng.sem_inc(passed, 1)

        def active(s, lag):
            return not isinstance(s, int) or lag <= s < lag + NCH

        def slot_steps(s):
            def go(step, lag, *which):
                if active(s, lag):
                    step(s - lag, *which)
            return go

        def run_slots(eng, slot):
            for s in range(LAST_LAG + 1):
                slot(s)
            with eng.Fori(LAST_LAG + 1, NCH) as s:
                slot(s)
            for s in range(NCH, SLOTS):
                slot(s)

        LOADS, SETUP = 7, 7
        block = ctx.enter_context(nc.Block())

        @block.sync
        def _(sp):
            x_rows = x.rearrange("(j b) t c -> b t j c", b=2)
            o_rows = out.rearrange("(j b) t c -> b t j c", b=2)

            def load_x(n):
                after(sp, s_norm, n)
                after(sp, s_xT, n)
                for half in range(2):
                    sp.dma_start(xtok[TC * half:TC * half + TC, :, :],
                                 x_rows[half, cols_tm(0, n)]).then_inc(s_x, 16)

            def store(j):
                sp.wait_ge(s_otok, j + 1)
                for half in range(2):
                    sp.dma_start(o_rows[half, cols(0, j)],
                                 otok[TC * half:TC * half + TC, :, :]).then_inc(s_out, 16)

            load_x(0)
            sp.dma_start(cst[:, :], consts).then_inc(s_params, 16)
            sp.dma_start(vec[:, :], vectors).then_inc(s_params, 16)
            sp.dma_start(boot[:, 0:U_ZERO], setup_only).then_inc(s_params, 16)
            sp.dma_start(wt[:, 0:W_QKV], weights[:, 0:W_QKV]).then_inc(s_params, 16)
            sp.dma_start(wt[:, W_QKV:W_ALL], weights[:, W_QKV:W_ALL]).then_inc(s_params, 16)
            sp.dma_start(b2e[:, :], b2_experts).then_inc(s_params, 16)
            sp.dma_start(pen[:, :], penalty_rows).then_inc(s_params, 16)

            def slot(s):
                if active(s, 0) and not (isinstance(s, int) and s == 0):
                    load_x(s)
                if active(s, LAST_LAG):
                    store(s - LAST_LAG)

            run_slots(sp, slot)
            sp.wait_ge(s_out, 32 * NCH)

        @block.gpsimd
        def _(pool):
            g = nc.gpsimd
            g.memset(kx[:, :, 0:1], NEG_INF)
            g.memset(ax[:, :, 0:1], 0.0)
            g.memset(bx[:, :, 0:1], 1.0)
            g.memset(alx[:, :, 0:1], 0.0)
            g.memset(bvx[:, :, 0:1], 0.0)
            g.memset(wrow[:, :, 0:1], NEG_INF)
            g.memset(eps_c[:, :], EPS).then_inc(s_pool0, 1)
            pool.wait_ge(s_params, 16 * LOADS)

            def tm_m(n):
                pool.wait_ge(s_m, n + 1)
                after(pool, s_d, n)
                g.tensor_tensor(ax[:, :, 1:TC + 1], mx[:, :, 0:TC], mx[:, :, 1:TC + 1], ALU.subtract).then_inc(s_am, 1)
                g.tensor_tensor(bx[:, :, 1:TC + 1], kx[:, :, 1:TC + 1], mx[:, :, 1:TC + 1], ALU.subtract).then_inc(s_bm, 1)
                g.tensor_copy(kx[:, :, 0:1], mx[:, :, TC:TC + 1]).then_inc(s_kcarry, 1)

            def tm_bb(n):
                pool.wait_ge(s_d, n + 1)
                own_wait(pool, s_passed_pool)
                g.tensor_copy(bx[:, :, 0:1], dx[:, :, TC:TC + 1]).then_inc(s_dcarry, 1)
                pool.wait_ge(s_lnd, n + 1)
                g.tensor_tensor(bbx[:, :, :], bbx[:, :, :], mx[:, :, :], ALU.add).then_inc(s_bb, 1)
                pool.wait_ge(s_bb, n + 1)
                after(pool, s_th, n)
                after(pool, s_t12, n)
                g.tensor_tensor(dl[:, :, :], bbx[:, :, 0:TC], kx[:, :, 1:TC + 1], ALU.subtract).then_inc(s_dl, 1)

            def tm_bv(n):
                pool.wait_ge(s_alpha, n + 1)
                pool.wait_ge(s_v, n + 1)
                g.tensor_tensor(bvx[:, :, 1:TC + 1], v3(t2[:, :]), vv[:, :, :], ALU.mult).then_inc(s_bv, 1)

            def tm_df(n):
                pool.wait_ge(s_aa, n + 1)
                after(pool, s_x2, n)
                g.tensor_tensor(df[:, :, :], aax[:, :, 0:TC], vv[:, :, :], ALU.subtract).then_inc(s_df, 1)
                g.tensor_copy(bvx[:, :, 0:1], aax[:, :, TC:TC + 1]).then_inc(s_aacarry, 1)

            def cm_xn(j):
                pool.wait_ge(s_nrm["c"], j + 1)
                own_wait(pool, s_passed_pool)
                g.tensor_scalar(xn[:, :], xn[:, :], V("g2"), V("b2"), ALU.mult, ALU.add).then_inc(s_xn, 1)

            def cm_xs(j):
                pool.wait_ge(s_x2, (j + 2) if not isinstance(j, int) else min(j + 2, NCH))
                after(pool, s_xres, j)
                g.tensor_tensor(xs[:, :, :], xres[:, :, cols(0, j)], x2[:, :, cols(1, j)], ALU.add).then_inc(s_xs, 1)

            def at_add(j, step):
                if step < 4:
                    pool.wait_ge(s_pv, 8 * j + 2 * step + 2)
                    a, b = prod[:, 2 * step, :], prod[:, 2 * step + 1, :]
                elif step == 4:
                    pool.wait_ge(s_add, 6 * j + 4)
                    p4 = prod[:, :, :].rearrange("p (u w) n -> p u w n", w=4)
                    a, b = p4[:, :, 0, :], p4[:, :, 2, :]
                else:
                    pool.wait_ge(s_add, 6 * j + 5)
                    a, b = prod[:, 0, :], prod[:, 4, :]
                g.tensor_tensor(a, a, b, ALU.add).then_inc(s_add, 1)

            def at_h(j):
                pool.wait_ge(s_nrm["h"], j + 1)
                after(pool, s_f5, j)
                after(pool, s_hlo, j)
                own_wait(pool, s_passed_pool)
                g.tensor_scalar(h[:, :], y4[:, :], V("g3"), V("b3"), ALU.mult, ALU.add).then_inc(s_h, 1)

            def at_hlo(j):
                pool.wait_ge(s_hhi, j + 1)
                g.tensor_tensor(h2[:, 1, :], h[:, :], h2[:, 0, :], ALU.subtract).then_inc(s_hlo, 1)

            def ex_out(j):
                pool.wait_ge(s_fa, j + 1)
                g.tensor_tensor(fo[:, :, :], fo[:, :, :], xres[:, :, cols(0, j)], ALU.add).then_inc(s_fo, 1)

            def slot(s):
                go = slot_steps(s)
                go(tm_m, 0)
                go(at_hlo, 4)
                go(tm_bb, 0)
                go(tm_bv, 0)
                go(at_add, 3, 0)
                go(at_add, 3, 1)
                go(tm_df, 0)
                go(at_add, 3, 2)
                go(at_add, 3, 3)
                go(at_add, 3, 4)
                go(at_add, 3, 5)
                go(ex_out, 4)
                go(cm_xs, 1)
                go(cm_xn, 1)
                go(at_h, 3)

            run_slots(pool, slot)

        @block.scalar
        def _(act):
            a = nc.scalar
            act.wait_ge(s_params, 16 * LOADS)
            act.wait_ge(s_pool0, 1)
            act.wait_ge(s_const, SETUP)
            eps = eps_c[:, 0:1]

            def table_gelu():
                a.preload_act_table_set("gelu_and_others")

            def table_exp():
                a.preload_act_table_set("natural_log_exp_and_others")

            def tm_stats(n):
                act.wait_ge(s_mv, n + 1)
                a.activation(ln_v[:, :], mv[:, :, 1], ACT.Ln, bias=eps).then_inc(s_r1, 1)
                act.wait_ge(s_r1, 3 * n + 1)
                after(act, s_norm, n)
                a.activation(inv_v[:, :], ln_v[:, :], ACT.Exp, scale=-1.0).then_inc(s_r1, 1)
                a.activation(r1[:, :], ln_v[:, :], ACT.Exp, scale=-0.5).then_inc(s_r1, 1)
                act.wait_ge(s_q2, n + 1)
                a.activation(ln_q[:, :], q2[:, :], ACT.Ln, bias=eps).then_inc(s_lnq, 1)
                act.wait_ge(s_lnvq, n + 1)
                a.activation(r12[:, :], ln_vq[:, :], ACT.Exp, scale=-0.5).then_inc(s_r12, 1)

            def tm_evac(n):
                act.wait_ge(s_xT, n + 1)
                a.copy(xres[:, :, cols_tm(0, n)], v3(pA[0][:, :])).then_inc(s_xTe, 1)
                act.wait_ge(s_xlT, n + 1)
                a.copy(xl[:, :, cols_tm(1, n)], v3(pA[1][:, :])).then_inc(s_xlTe, 1)
                if isinstance(n, int) and n == 0:
                    a.copy(xl[:, :, 0:1], v3(pA[1][:, :])[:, :, 0:1]).then_inc(s_prev0, 1)
                act.wait_ge(s_zT, n + 1)
                after(act, s_rps, n)
                a.activation(z[:, :], pA[0][:, :], ACT.Identity, scale=V("g1"), bias=V("b1")).then_inc(s_zTe, 1)

            def tm_ab(n):
                act.wait_ge(s_am, n + 1)
                a.activation(ax[:, :, 1:TC + 1], ax[:, :, 1:TC + 1], ACT.Exp, bias=V("w"))
                act.wait_ge(s_bm, n + 1)
                a.activation(bx[:, :, 1:TC + 1], bx[:, :, 1:TC + 1], ACT.Exp).then_inc(s_ab, 1)

            def tm_lnd(n):
                act.wait_ge(s_d, n + 1)
                after(act, s_dl, n)
                a.activation(bbx[:, :, :], dx[:, :, :], ACT.Ln).then_inc(s_lnd, 1)

            def tm_alpha(n):
                act.wait_ge(s_t12, n + 1)
                after(act, s_aa, n)
                a.activation(alx[:, :, 1:TC + 1], v3(t1[:, :]), ACT.Exp)
                a.activation(t2[:, :], t2[:, :], ACT.Exp, scale=-1.0).then_inc(s_alpha, 1)

            def tm_tanh(n):
                act.wait_ge(s_t12, n + 1)
                act.wait_ge(s_dl, n + 1)
                a.activation(dl[:, :, :], dl[:, :, :], ACT.Tanh, scale=0.5, bias=half_u[:, 0:1])
                act.wait_ge(s_r, n + 1)
                a.activation(rr[:, :, :], rr[:, :, :], ACT.Tanh, scale=0.5).then_inc(s_th, 1)

            centred = {"c": pA[0], "a": pB[0], "h": pC[0], "e": pC[0]}
            variance = {"c": pA[1], "a": pB[1], "h": pC[1], "e": pC[1]}

            def ln_square(j, st):
                act.wait_ge(s_cen[st], j + 1)
                after(act, s_nrm[st], j)
                a.activation(sqr[st][:, :], centred[st][:, :], ACT.Square).then_inc(s_sq[st], 1)

            def ln_rstd(j, st):
                act.wait_ge(s_var[st], j + 1)
                a.activation(rstd[st][:, :], variance[st][:, :], ACT.Ln, bias=eps).then_inc(s_lnr[st], 1)
                act.wait_ge(s_lnr[st], j + 1)
                a.activation(rstd[st][:, :], rstd[st][:, :], ACT.Exp, scale=-0.5).then_inc(s_rstd[st], 1)

            def cm_tanh(j):
                act.wait_ge(s_tr, j + 1)
                a.activation(xpr[:, :, :], xpr[:, :, :], ACT.Tanh, scale=0.5).then_inc(s_thc, 1)

            def at_qkv(j, i):
                act.wait_ge(s_qkvps, 3 * j + i + 1)
                if i < 2:
                    after(act, s_prod, 4 * j)
                else:
                    after(act, s_pv, 8 * j)
                a.activation(qkv[:, i, :], pB[i % 2][:, :] if i else pB[0][:, :], ACT.Identity,
                             bias=V(("bq", "bk", "bv")[i])).then_inc(s_qkv, 1)

            def at_exp(j):
                act.wait_ge(s_sm, j + 1)
                a.activation(pr[:, :, :, :], pr[:, :, :, :], ACT.Exp, scale=ATT_SCALE).then_inc(s_pr, 1)

            def at_st(j):
                act.wait_ge(s_score, j + 1)
                after(act, s_sT, j)
                a.copy(st[:, :], pB[1][:, :]).then_inc(s_st, 1)

            def at_attn(j):
                act.wait_ge(s_aT, j + 1)
                after(act, s_exp, 8 * j)
                after(act, s_attn, j)
                a.copy(attn[:, 0, :], pB[1][:, :]).then_inc(s_ahi, 1)

            def at_hhi(j):
                act.wait_ge(s_h, j + 1)
                after(act, s_moe, 8 * j)
                a.copy(h2[:, 0, :], h[:, :]).then_inc(s_hhi, 1)

            def at_mask(j):
                act.wait_ge(s_maskps, j + 1)
                after(act, s_moe, 8 * j)
                rows = pC[1][:, :].bitcast(BF16)[0:E, 0:N]
                a.copy(maskt[:, :], rows)
                a.activation(unmask[:, :], rows, ACT.Identity, scale=-1.0,
                             bias=1.0).then_inc(s_maskt, 1)

            def ex_gelu(j, e):
                act.wait_ge(s_pre, 8 * j + e + 1)
                after(act, s_moe, 8 * j + e - 1)
                a.activation(he[:, e % 2, :], pC[e % 2][:, :], ACT.Gelu, bias=V(f"be{e}")).then_inc(s_he, 1)

            def ex_affine(j):
                act.wait_ge(s_nrm["e"], j + 1)
                after(act, s_oT, j)
                a.activation(fo[:, :, :], v3(f5[:, :]), ACT.Identity, scale=V("g4"), bias=V("b4")).then_inc(s_fa, 1)

            def ex_store(j):
                act.wait_ge(s_oT, j + 1)
                after(act, s_out, 32 * j)
                a.copy(otok[:, :, :], pC[0][:, :].rearrange("p (j c) -> p j c", c=C)).then_inc(s_otok, 1)

            def slot(s):
                go = slot_steps(s)
                go(at_attn, 4)
                table_exp()
                go(tm_alpha, 1)
                table_gelu()
                go(ex_gelu, 5, 4)
                go(ex_gelu, 5, 5)
                go(ex_gelu, 5, 6)
                go(cm_tanh, 3)
                go(tm_tanh, 1)
                go(ex_gelu, 5, 7)
                go(ln_square, 5, "e")
                table_exp()
                go(tm_stats, 0)
                go(ln_rstd, 5, "e")
                go(ln_square, 2, "c")
                go(ln_square, 3, "a")
                go(ex_affine, 5)
                go(ex_store, 5)
                go(ln_rstd, 3, "a")
                go(ln_rstd, 2, "c")
                go(ln_square, 4, "h")
                go(at_qkv, 3, 0)
                go(ln_rstd, 4, "h")
                go(at_qkv, 3, 1)
                go(tm_evac, 0)
                go(at_qkv, 3, 2)
                go(at_hhi, 4)
                go(at_mask, 4)
                table_gelu()
                go(ex_gelu, 4, 0)
                go(at_st, 3)
                go(ex_gelu, 4, 1)
                table_exp()
                go(tm_ab, 0)
                go(at_exp, 3)
                go(tm_lnd, 0)
                table_gelu()
                go(ex_gelu, 4, 2)
                go(ex_gelu, 4, 3)

            table_gelu()
            run_slots(act, slot)

        @block.vector
        def _(dve):
            v = nc.vector
            dve.wait_ge(s_params, 16 * LOADS)
            dve.wait_ge(s_pool0, 1)
            v.tensor_scalar(om[:, 0:3], vec[:, VI["tmk"]:VI["tmk"] + 3], -1.0, 1.0, ALU.mult, ALU.add)
            v.tensor_scalar(om[:, 3:5], vec[:, VI["cmk"]:VI["cmk"] + 2], -1.0, 1.0, ALU.mult, ALU.add)
            v.tensor_scalar(half_u[:, :], V("u"), -0.5, None, ALU.mult).then_inc(s_const, 1)
            v.memset(boot[:, U_ZERO:U_ZERO + N], 0.0).then_inc(s_const, 1)
            v.tensor_tensor(wt[:, W_TM:W_TM + 3 * C], wt[:, W_TM:W_TM + 3 * C], boot[:, U_ROWS:U_ROWS + 3 * C],
                            ALU.mult).then_inc(s_const, 1)
            v.tensor_tensor(wt[:, W_CM:W_CM + FF * C].rearrange("p (f c) -> p f c", f=FF),
                            wt[:, W_CM:W_CM + FF * C].rearrange("p (f c) -> p f c", f=FF),
                            boot[:, U_ROWS + 3 * C:U_ROWS + 4 * C].unsqueeze(1).broadcast_to([128, FF, C]),
                            ALU.mult).then_inc(s_const, 1)
            v.tensor_copy(ident16[:, :], ident)
            v.tensor_copy(spread[:, :], boot[:, U_SPREAD:U_SPREAD + B * C])
            v.tensor_copy(w1[:, 0, :], boot[:, U_W1:U_W1 + E * C]).then_inc(s_const, 1)
            dve.wait_ge(s_const, 5)
            v.tensor_tensor(w1[:, 1, :], boot[:, U_W1:U_W1 + E * C], w1[:, 0, :], ALU.subtract).then_inc(s_const, 1)
            v.tensor_scalar(wrow[:, :, 1:TC + 1], v3(boot[:, U_ZERO:U_ZERO + N]), V("w"), None, ALU.add).then_inc(s_const, 1)
            dve.wait_ge(s_const, SETUP)

            def tm_stats(n):
                dve.wait_ge(s_x, 32 * n + 32)
                for i in range(TILES):
                    ins = v.bn_stats(stats[:, i, :], xtok[:, i, :])
                ins.then_inc(s_stats, 1)
                dve.wait_ge(s_stats, n + 1)
                own_wait(dve, s_passed_dve)
                for i in range(TILES):
                    ins = v.bn_aggr(mv[:, i, :], stats[:, i, :])
                ins.then_inc(s_mv, 1)

            def tm_q2(n):
                dve.wait_ge(s_r1, 3 * n + 2)
                v.tensor_tensor(q2[:, :], mv[:, :, 1], inv_v[:, :], ALU.mult).then_inc(s_q2, 1)
                dve.wait_ge(s_lnq, n + 1)
                v.tensor_tensor(ln_vq[:, :], ln_v[:, :], ln_q[:, :], ALU.add).then_inc(s_lnvq, 1)

            def tm_norm(n):
                dve.wait_ge(s_r1, 3 * n + 3)
                dve.wait_ge(s_r12, n + 1)
                after(dve, s_zT, n)
                for i in range(TILES):
                    v.tensor_scalar(xltok[:, i, :], xtok[:, i, :], mv[:, i, 0:1], r1[:, i:i + 1],
                                    ALU.subtract, ALU.mult)
                    ins = v.tensor_scalar(ztok[:, i, :], xtok[:, i, :], mv[:, i, 0:1], r12[:, i:i + 1],
                                          ALU.subtract, ALU.mult)
                ins.then_inc(s_norm, 1)

            def tm_k(n):
                dve.wait_ge(s_xlTe, n + 1)
                dve.wait_ge(s_prev0, 1)
                dve.wait_ge(s_kps, n + 1)
                after(dve, s_dl, n)
                v.scalar_tensor_tensor(kx[:, :, 1:TC + 1], xl[:, :, cols_tm(0, n)], om[:, 0:1], v3(pA[1][:, :]),
                                       ALU.mult, ALU.add).then_inc(s_k, 1)

            def tm_v(n):
                dve.wait_ge(s_vps, n + 1)
                after(dve, s_bv, n)
                after(dve, s_df, n)
                v.scalar_tensor_tensor(vv[:, :, :], xl[:, :, cols_tm(0, n)], om[:, 1:2], v3(pA[0][:, :]),
                                       ALU.mult, ALU.add).then_inc(s_v, 1)

            def tm_r(n):
                dve.wait_ge(s_rps, n + 1)
                v.scalar_tensor_tensor(rr[:, :, :], xl[:, :, cols_tm(0, n)], om[:, 2:3], v3(pA[1][:, :]),
                                       ALU.mult, ALU.add).then_inc(s_r, 1)

            def tm_mscan(n):
                dve.wait_ge(s_k, n + 1)
                after(dve, s_kcarry, n)
                after(dve, s_bb, n)
                after(dve, s_bm, n)
                v.tensor_tensor_scan(mx[:, :, :].rearrange("p b t -> p (b t)"),
                                     wrow[:, :, :].rearrange("p b t -> p (b t)"),
                                     kx[:, :, :].rearrange("p b t -> p (b t)"), NEG_INF,
                                     ALU.add, ALU.max).then_inc(s_m, 1)

            def tm_d(n):
                dve.wait_ge(s_ab, n + 1)
                after(dve, s_dcarry, n)
                after(dve, s_lnd, n)
                v.tensor_tensor_scan(dx[:, :, :].rearrange("p b t -> p (b t)"),
                                     ax[:, :, :].rearrange("p b t -> p (b t)"),
                                     bx[:, :, :].rearrange("p b t -> p (b t)"), 0.0,
                                     ALU.mult, ALU.add).then_inc(s_d, 1)

            def tm_t12(n):
                dve.wait_ge(s_dl, n + 1)
                after(dve, s_bv, n)
                v.tensor_scalar(v3(t1[:, :]), dl[:, :, :], V("w"), 0.0, ALU.add, ALU.min)
                v.tensor_scalar(v3(t2[:, :]), dl[:, :, :], V("w"), 0.0, ALU.add, ALU.max).then_inc(s_t12, 1)

            def tm_aa(n):
                dve.wait_ge(s_bv, n + 1)
                after(dve, s_aacarry, n)
                v.tensor_tensor_scan(aax[:, :, :].rearrange("p b t -> p (b t)"),
                                     alx[:, :, :].rearrange("p b t -> p (b t)"),
                                     bvx[:, :, :].rearrange("p b t -> p (b t)"), 0.0,
                                     ALU.mult, ALU.add).then_inc(s_aa, 1)

            def tm_y(n):
                dve.wait_ge(s_df, n + 1)
                dve.wait_ge(s_th, n + 1)
                v.scalar_tensor_tensor(ty[:, :, :], dl[:, :, :], 1.0, df[:, :, :],
                                       ALU.add, ALU.mult).then_inc(s_ysteps, 1)
                dve.wait_ge(s_ysteps, 3 * n + 1)
                v.scalar_tensor_tensor(ty[:, :, :], vv[:, :, :], 2.0, ty[:, :, :],
                                       ALU.mult, ALU.add).then_inc(s_ysteps, 1)
                dve.wait_ge(s_ysteps, 3 * n + 2)
                v.scalar_tensor_tensor(ty[:, :, :], rr[:, :, :], 1.0, ty[:, :, :],
                                       ALU.add, ALU.mult).then_inc(s_ysteps, 1)
                dve.wait_ge(s_ysteps, 3 * n + 3)
                v.scalar_tensor_tensor(x2[:, :, cols_tm(1, n)], ty[:, :, :], 0.25, xl[:, :, cols_tm(1, n)],
                                       ALU.mult, ALU.add).then_inc(s_x2, 1)

            def tm_wrap():
                dve.wait_ge(s_x2, NCH)
                v.tensor_copy(x2[:, :, 0:1], x2[:, :, T:T + 1]).then_inc(s_wrap, 1)

            def ln_scale(st, cen, dst, j):
                dve.wait_ge(s_rstd[st], j + 1)
                v.tensor_tensor(dst[:, :], cen[:, :], rstd[st][:, :], ALU.mult).then_inc(s_nrm[st], 1)

            def cm_scale(j):
                after(dve, s_tr, j)
                after(dve, s_kk, 4 * j)
                ln_scale("c", pA[0], xn, j)

            def cm_prev(j):
                if isinstance(j, int) and j == NCH - 1:
                    dve.wait_ge(s_wrap, 1)
                prev = x2[:, :, cols(0, j)]
                after(dve, s_o1, j)
                after(dve, s_kkm, 4 * j)
                v.tensor_scalar(xpk[:, :, :], prev, om[:, 3:4], None, ALU.mult)
                v.tensor_scalar(xpr[:, :, :], prev, om[:, 4:5], None, ALU.mult).then_inc(s_xp, 1)

            def cm_gate(j):
                dve.wait_ge(s_xn, j + 1)
                dve.wait_ge(s_xp, j + 1)
                v.scalar_tensor_tensor(xpr[:, :, :], v3(xn[:, :]), V("cmr"), xpr[:, :, :],
                                       ALU.mult, ALU.add).then_inc(s_tr, 1)

            def cm_hidden(j, f):
                dve.wait_ge(s_kk, 4 * j + f + 1)
                dve.wait_ge(s_xp, j + 1)
                after(dve, s_kk2, 4 * j + f - 1)
                v.tensor_tensor(v3(kk[:, f % 2, :]), v3(pA[f % 2][:, :]), xpk[:, :, :], ALU.add).then_inc(s_kkm, 1)
                dve.wait_ge(s_kkm, 4 * j + f + 1)
                after(dve, s_vvps, j)
                v.scalar_tensor_tensor(kk2[:, f, :], kk[:, f % 2, :], 0.0, kk[:, f % 2, :],
                                       ALU.max, ALU.mult).then_inc(s_kk2, 1)

            def cm_out(j):
                dve.wait_ge(s_thc, j + 1)
                dve.wait_ge(s_vvps, j + 1)
                v.scalar_tensor_tensor(xpr[:, :, :], xpr[:, :, :], 1.0, v3(pAcc[:, :]),
                                       ALU.add, ALU.mult).then_inc(s_o1, 1)
                dve.wait_ge(s_o1, j + 1)
                dve.wait_ge(s_xs, j + 1)
                v.scalar_tensor_tensor(xres[:, :, cols(0, j)], xpr[:, :, :], 0.5, xs[:, :, :],
                                       ALU.mult, ALU.add).then_inc(s_xres, 1)

            def at_scale(j):
                after(dve, s_y4, j)
                ln_scale("a", pB[0], x3, j)

            def at_prod(j, i):
                dve.wait_ge(s_qkv, 3 * j + 2)
                after(dve, s_add, 6 * j)
                after(dve, s_ops, j)
                q = v3(qkv[:, 0, :]).unsqueeze(1).broadcast_to([128, 2, B, TC])
                k = v3(qkv[:, 1, :])[:, 2 * i:2 * i + 2, :].unsqueeze(2).broadcast_to([128, 2, B, TC])
                v.tensor_tensor(prod[:, 2 * i:2 * i + 2, :].rearrange("p s (b t) -> p s b t", b=B), q, k,
                                ALU.mult).then_inc(s_prod, 1)

            def at_softmax_in(j):
                dve.wait_ge(s_sT, j + 1)
                S = pB[0][:, :].rearrange("p (j s h) -> p j s h", j=TILES, s=B)
                v.tensor_reduce(smax[:, :, :], S.rearrange("p j s h -> p j h s"), X, ALU.max).then_inc(s_smax, 1)
                dve.wait_ge(s_smax, j + 1)
                after(dve, s_aT, j)
                v.tensor_tensor(pr[:, :, :, :], S, smax[:, :, :].unsqueeze(2).broadcast_to([128, TILES, B, H]),
                                ALU.subtract).then_inc(s_sm, 1)

            def at_softmax_out(j):
                dve.wait_ge(s_pr, j + 1)
                v.tensor_reduce(ssum[:, :, :], pr[:, :, :, :].rearrange("p j s h -> p j h s"), X,
                                ALU.add).then_inc(s_ssum, 1)
                dve.wait_ge(s_ssum, j + 1)
                v.reciprocal(sinv[:, :, :], ssum[:, :, :]).then_inc(s_sinv, 1)
                dve.wait_ge(s_sinv, j + 1)
                v.tensor_tensor(pr[:, :, :, :], pr[:, :, :, :],
                                sinv[:, :, :].unsqueeze(2).broadcast_to([128, TILES, B, H]),
                                ALU.mult).then_inc(s_a, 1)

            def at_alo(j):
                dve.wait_ge(s_ahi, j + 1)
                v.tensor_tensor(attn[:, 1, :], pB[1][:, :], attn[:, 0, :], ALU.subtract).then_inc(s_attn, 1)

            def at_pv(j, s):
                dve.wait_ge(s_exp, 8 * j + s + 1)
                if s == 0:
                    dve.wait_ge(s_qkv, 3 * j + 3)
                val = v3(qkv[:, 2, :])[:, s:s + 1, :].broadcast_to([128, B, TC])
                v.tensor_tensor(v3(prod[:, s, :]), v3(pB[s % 2][:, :]), val, ALU.mult).then_inc(s_pv, 1)

            def at_y(j):
                dve.wait_ge(s_ops, j + 1)
                after(dve, s_h, j)
                v.scalar_tensor_tensor(y4[:, :], pAcc[:, :], V("bo"), x3[:, :], ALU.add, ALU.add).then_inc(s_y4, 1)

            def at_h(j):
                dve.wait_ge(s_cen["h"], j + 1)
                ln_scale("h", pC[0], y4, j)

            def at_logits(j):
                dve.wait_ge(s_lgps, j + 1)
                v.tensor_tensor(lg[:, :, :], pC[0][:, 0:TILES * E].rearrange("p (j e) -> p j e", e=E),
                                router_bias.unsqueeze(1).broadcast_to([128, TILES, E]),
                                ALU.add).then_inc(s_lgsteps, 1)
                dve.wait_ge(s_lgsteps, 4 * j + 1)
                v.tensor_reduce(lmax[:, :], lg[:, :, :], X, ALU.max).then_inc(s_lgsteps, 1)
                dve.wait_ge(s_lgsteps, 4 * j + 2)
                v.tensor_tensor(lg[:, :, :], lg[:, :, :], lmax[:, :].unsqueeze(2).broadcast_to([128, TILES, E]),
                                ALU.subtract).then_inc(s_lgsteps, 1)
                dve.wait_ge(s_lgsteps, 4 * j + 3)
                v.tensor_scalar(lg[:, :, :], lg[:, :, :], EXP_IS_ZERO, None, ALU.max).then_inc(s_lgsteps, 1)

            def at_route(j):
                dve.wait_ge(s_lgsteps, 4 * j + 4)
                own_wait(dve, s_passed_dve)
                for i in range(TILES):
                    ins = v.max(top[:, i, :], lg[:, i, :])
                ins.then_inc(s_top, 1)
                dve.wait_ge(s_top, 2 * j + 1)
                own_wait(dve, s_passed_dve)
                for i in range(TILES):
                    ins = v.max_index(topi[:, i, :], top[:, i, :], lg[:, i, :])
                ins.then_inc(s_top, 1)
                dve.wait_ge(s_top, 2 * j + 2)
                v.tensor_tensor(assign[:, :], topi[:, :, 0], topi[:, :, 1], ALU.max).then_inc(s_assign, 1)
                dve.wait_ge(s_assign, j + 1)
                after(dve, s_maskps, j)
                v.tensor_tensor(mask[:, :, :], cst[:, K_IOTA:K_IOTA + TILES * E].rearrange("p (j e) -> p j e", e=E),
                                assign[:, :].unsqueeze(2).broadcast_to([128, TILES, E]),
                                ALU.is_equal).then_inc(s_mask, 1)

            def ex_sum(j):
                dve.wait_ge(s_moe, 8 * j + 8)
                after(dve, s_fa, j)
                v.tensor_tensor(f5[:, :], pMoe[:, :], h[:, :], ALU.add).then_inc(s_f5, 1)

            def ex_scale(j):
                dve.wait_ge(s_cen["e"], j + 1)
                ln_scale("e", pC[0], f5, j)

            def slot(s):
                go = slot_steps(s)
                go(tm_r, 1)
                go(at_logits, 5)
                go(at_route, 5)
                go(at_prod, 4, 2)
                go(cm_prev, 3)
                go(at_prod, 4, 3)
                go(tm_stats, 0)
                if isinstance(s, int) and s == NCH - 1 + 2:
                    tm_wrap()
                go(cm_gate, 3)
                go(cm_hidden, 3, 0)
                go(at_softmax_in, 4)
                go(tm_d, 1)
                go(cm_hidden, 3, 1)
                go(at_softmax_out, 4)
                go(cm_hidden, 3, 2)
                go(tm_t12, 1)
                go(at_alo, 4)
                go(cm_hidden, 3, 3)
                go(at_pv, 4, 0)
                go(at_pv, 4, 1)
                go(at_pv, 4, 2)
                go(at_pv, 4, 3)
                go(tm_aa, 1)
                go(at_pv, 4, 4)
                go(at_pv, 4, 5)
                go(ex_sum, 5)
                go(at_pv, 4, 6)
                go(at_pv, 4, 7)
                go(tm_y, 1)
                go(cm_out, 3)
                go(tm_q2, 0)
                go(ex_scale, 5)
                go(at_y, 4)
                go(tm_norm, 0)
                go(at_scale, 3)
                go(cm_scale, 2)
                go(at_h, 4)
                go(at_prod, 3, 0)
                go(at_prod, 3, 1)
                go(tm_k, 0)
                go(tm_v, 0)
                go(tm_mscan, 0)

            run_slots(dve, slot)

        @block.tensor
        def _(pe):
            t = nc.tensor
            pe.wait_ge(s_params, 16 * LOADS)
            pe.wait_ge(s_const, SETUP)

            def transposes(dst, src, done):
                for i in range(TILES):
                    ins = t.transpose(dst[:, 128 * i:128 * i + 128], src[:, i, :], ident)
                ins.then_inc(done, 1)

            def ln_centre(st, dst, src, j):
                t.matmul(dst, centre, src, start=True, stop=True).then_inc(s_cen[st], 1)

            variance = {"c": pA[1], "a": pB[1], "h": pC[1], "e": pC[1]}

            def ln_var(j, st):
                pe.wait_ge(s_sq[st], j + 1)
                t.matmul(variance[st][:, :], mean, sqr[st][:, :], start=True, stop=True).then_inc(s_var[st], 1)

            def tm_transpose(n, i):
                if i == 0:
                    pe.wait_ge(s_norm, n + 1)
                    if not isinstance(n, int) or n >= AHEAD:
                        pe.wait_ge(s_nrm["c"], n - 1)
                    else:
                        after(pe, s_v, n)
                        after(pe, s_r, n)
                    transposes(pA[0], xtok, s_xT)
                elif i == 1:
                    transposes(pA[1], xltok, s_xlT)
                else:
                    pe.wait_ge(s_xTe, n + 1)
                    transposes(pA[0], ztok, s_zT)

            def tm_kv(n):
                pe.wait_ge(s_zTe, n + 1)
                pe.wait_ge(s_xlTe, n + 1)
                if isinstance(n, int) and n == 0:
                    pe.wait_ge(s_prev0, 1)
                t.matmul(pA[1][:, :], wt[:, W_TM:W_TM + C], z[:, :], start=True, stop=True).then_inc(s_kps, 1)
                t.matmul(pA[0][:, :], wt[:, W_TM + C:W_TM + 2 * C], z[:, :], start=True,
                         stop=True).then_inc(s_vps, 1)

            def tm_r(n):
                pe.wait_ge(s_k, n + 1)
                t.matmul(pA[1][:, :], wt[:, W_TM + 2 * C:W_TM + 3 * C], z[:, :], start=True,
                         stop=True).then_inc(s_rps, 1)

            def cm_centre(j):
                if isinstance(j, int) and j == 0:
                    pe.wait_ge(s_v, AHEAD)
                    pe.wait_ge(s_r, AHEAD)
                pe.wait_ge(s_x2, (j + 2) if not isinstance(j, int) else min(j + 2, NCH))
                after(pe, s_kkm, 4 * j)
                ln_centre("c", v3(pA[0][:, :]), x2[:, :, cols(1, j)], j)

            def cm_hidden(j, f):
                if f == 0:
                    pe.wait_ge(s_xn, j + 1)
                    if not isinstance(j, int) or j + AHEAD < NCH:
                        pe.wait_ge(s_v, j + AHEAD + 1)
                        pe.wait_ge(s_r, j + AHEAD + 1)
                if f >= 2:
                    pe.wait_ge(s_kkm, 4 * j + f - 1)
                t.matmul(pA[f % 2][:, :], wt[:, W_CM + f * C:W_CM + f * C + C], xn[:, :], start=True,
                         stop=True).then_inc(s_kk, 1)

            def cm_mlp(j, f):
                if f == 0:
                    after(pe, s_y4, j - 1)
                    after(pe, s_o1, j)
                pe.wait_ge(s_kk2, 4 * j + f + 1)
                ins = t.matmul(pAcc[:, :], wt[:, W_CP + f * C:W_CP + f * C + C], kk2[:, f, :],
                               start=(f == 0), stop=(f == FF - 1))
                if f == FF - 1:
                    ins.then_inc(s_vvps, 1)

            def at_centre(j):
                pe.wait_ge(s_xres, j + 1)
                after(pe, s_pv, 8 * j)
                ln_centre("a", v3(pB[0][:, :]), xres[:, :, cols(0, j)], j)

            def at_q(j):
                pe.wait_ge(s_nrm["a"], j + 1)
                t.matmul(pB[0][:, :], wt[:, W_QKV:W_QKV + C], x3[:, :], start=True, stop=True).then_inc(s_qkvps, 1)

            def at_kv(j):
                t.matmul(pB[1][:, :], wt[:, W_QKV + C:W_QKV + 2 * C], x3[:, :], start=True,
                         stop=True).then_inc(s_qkvps, 1)
                pe.wait_ge(s_qkv, 3 * j + 1)
                t.matmul(pB[0][:, :], wt[:, W_QKV + 2 * C:W_QKV + 3 * C], x3[:, :], start=True,
                         stop=True).then_inc(s_qkvps, 1)

            def at_scores(j, i):
                pe.wait_ge(s_prod, 4 * j + i + 1)
                for odd in range(2):
                    ins = t.matmul(pB[1][32 * i:32 * i + 32, :],
                                   cst[:, K_HEADS + 2 * H * odd:K_HEADS + 2 * H * odd + 2 * H],
                                   prod[:, 2 * i + odd, :], start=(odd == 0), stop=(odd == 1))
                if i == 3:
                    ins.then_inc(s_score, 1)

            def at_st(j):
                pe.wait_ge(s_st, j + 1)
                pe.wait_ge(s_qkv, 3 * j + 3)
                transposes(pB[0], st[:, :].rearrange("p (j n) -> p j n", n=128), s_sT)

            def at_transpose(j):
                pe.wait_ge(s_a, j + 1)
                transposes(pB[1], pr[:, :, :, :].rearrange("p j s h -> p j (s h)"), s_aT)

            def at_expand(j, s):
                if s == 0:
                    pe.wait_ge(s_attn, j + 1)
                if s >= 2:
                    pe.wait_ge(s_pv, 8 * j + s - 1)
                for part in range(2):
                    ins = t.matmul(pB[s % 2][:, :], spread[:, s * 128:s * 128 + 128], attn[:, part, :],
                                   start=(part == 0), stop=(part == 1))
                ins.then_inc(s_exp, 1)

            def at_out(j):
                pe.wait_ge(s_add, 6 * j + 6)
                if not isinstance(j, int) or j + 1 < NCH:
                    pe.wait_ge(s_o1, j + 2)
                t.matmul(pAcc[:, :], wt[:, W_OUT:W_OUT + C], prod[:, 0, :], start=True, stop=True).then_inc(s_ops, 1)

            def at_centre2(j):
                pe.wait_ge(s_y4, j + 1)
                after(pe, s_otok, j)
                ln_centre("h", pC[0][:, :], y4[:, :], j)

            def at_router(j):
                pe.wait_ge(s_h, j + 1)
                for i in range(TILES):
                    ins = t.matmul(pC[0][:, E * i:E * i + E], h[:, 128 * i:128 * i + 128],
                                   wt[:, W_ROUTER:W_ROUTER + E], start=True, stop=True)
                ins.then_inc(s_lgps, 1)

            def at_mask(j):
                pe.wait_ge(s_mask, j + 1)
                for i in range(TILES):
                    ins = t.transpose(pC[1][:, :].bitcast(BF16)[0:E, 128 * i:128 * i + 128], mask[:, i, :],
                                      ident16[:, :])
                ins.then_inc(s_maskps, 1)

            def ex_in(j, e):
                if e == 0:
                    pe.wait_ge(s_maskt, j + 1)
                    pe.wait_ge(s_hlo, j + 1)
                if e >= 2:
                    pe.wait_ge(s_he, 8 * j + e - 1)
                for wp, hp in ((0, 0), (0, 1), (1, 0)):
                    t.matmul(pC[e % 2][:, :], w1[:, wp, e * C:e * C + C], h2[:, hp, :], start=(wp + hp == 0),
                             stop=False)
                t.matmul(pC[e % 2][:, :], pen[:, e * C:e * C + C], unmask[:, :], start=False,
                         stop=True).then_inc(s_pre, 1)

            def ex_out(j, e):
                pe.wait_ge(s_he, 8 * j + e + 1)
                if e == 0:
                    after(pe, s_f5, j)
                    t.matmul(pMoe[:, :], b2e[:, :], maskt[:, :], start=True, stop=False)
                t.matmul(pMoe[:, :], wt[:, W_2 + e * C:W_2 + e * C + C], he[:, e % 2, :], start=False,
                         stop=(e == E - 1)).then_inc(s_moe, 1)

            def ex_centre(j):
                pe.wait_ge(s_f5, j + 1)
                ln_centre("e", pC[0][:, :], f5[:, :], j)

            def ex_transpose(j):
                pe.wait_ge(s_fo, j + 1)
                transposes(pC[0], fo[:, :, :].rearrange("p (j b) t -> p j (b t)", b=2), s_oT)

            def slot(s):
                go = slot_steps(s)
                go(ln_var, 5, "e")
                go(cm_centre, 2)
                go(at_centre, 3)
                go(at_out, 4)
                go(ln_var, 3, "a")
                go(ex_transpose, 5)
                go(ln_var, 2, "c")
                go(at_centre2, 4)
                go(at_q, 3)
                go(ln_var, 4, "h")
                go(tm_transpose, 0, 0)
                go(at_kv, 3)
                go(tm_transpose, 0, 1)
                go(tm_transpose, 0, 2)
                go(at_router, 4)
                go(tm_kv, 0)
                go(tm_r, 0)
                go(at_scores, 3, 0)
                go(cm_hidden, 2, 0)
                go(at_mask, 4)
                go(at_scores, 3, 1)
                go(cm_hidden, 2, 1)
                go(ex_in, 4, 0)
                go(at_scores, 3, 2)
                go(ex_in, 4, 1)
                go(at_scores, 3, 3)
                go(ex_out, 4, 0)
                go(at_st, 3)
                go(cm_hidden, 2, 2)
                go(ex_out, 4, 1)
                go(ex_in, 4, 2)
                go(ex_in, 4, 3)
                go(cm_hidden, 2, 3)
                go(ex_in, 4, 4)
                go(at_transpose, 3)
                go(cm_mlp, 2, 0)
                go(ex_in, 4, 5)
                go(ex_out, 4, 2)
                go(at_expand, 3, 0)
                go(ex_out, 4, 3)
                go(at_expand, 3, 1)
                go(cm_mlp, 2, 1)
                go(at_expand, 3, 2)
                go(ex_out, 4, 4)
                go(at_expand, 3, 3)
                go(ex_in, 4, 6)
                go(ex_out, 4, 5)
                go(ex_in, 4, 7)
                go(at_expand, 3, 4)
                go(ex_out, 4, 6)
                go(at_expand, 3, 5)
                go(ex_out, 4, 7)
                go(at_expand, 3, 6)
                go(at_expand, 3, 7)
                go(cm_mlp, 2, 2)
                go(ex_centre, 4)
                go(cm_mlp, 2, 3)

            run_slots(pe, slot)


def kernel(**inputs):
    import ml_dtypes
    import numpy as np
    import concourse.bacc as bacc
    from concourse.bass_utils import run_bass_kernel_spmd

    a = {k: np.asarray(v) for k, v in inputs.items()}
    A = {k[8:]: v for k, v in a.items() if k.startswith("L0_attn_")}
    Fm = {k[7:]: v for k, v in a.items() if k.startswith("L0_ffn_")}
    f = np.float32

    weights = np.concatenate([
        A["W_tm"], A["W_cm"],
        A["W_cp"].reshape(FF, C, C).transpose(1, 0, 2).reshape(C, FF * C),
        Fm["in_proj_w"].T, Fm["out_w"].T, Fm["router_w"].T,
        Fm["w2"].transpose(2, 0, 1).reshape(C, E * C)], axis=1)
    ib = Fm["in_proj_b"].reshape(3, C)
    cols = [A["time_decay"], A["time_first"], A["g1"], A["b1"], A["tmk"].reshape(C), A["tmv"].reshape(C),
            A["tmr"].reshape(C), A["g2"], A["b2"], A["cmk"].reshape(C), A["cmr"].reshape(C),
            ib[0], ib[1], ib[2], Fm["out_b"], Fm["ln1_g"], Fm["ln1_b"], Fm["ln2_g"], Fm["ln2_b"]]
    vectors = np.stack(cols + [Fm["b1"][e] for e in range(E)], axis=1)
    rows = np.concatenate([A["tmk"].reshape(C), A["tmv"].reshape(C), A["tmr"].reshape(C), A["cmk"].reshape(C)])

    eye = np.eye(128, dtype=f)
    average = np.full((128, 128), 1.0 / C, f)
    heads = np.repeat(np.eye(H, dtype=f), D, axis=0)
    iota = np.broadcast_to(np.tile(np.arange(E, dtype=f), TILES)[None, :], (128, TILES * E))
    expand = np.zeros((B, H, B, C), f)
    for s in range(B):
        expand[s, :, s, :] = heads.T
    none = np.zeros_like(heads)
    consts = np.concatenate([eye, eye - average, average, heads, none, none, heads, iota,
                             np.broadcast_to(Fm["router_b"][None, :], (128, E))], axis=1)
    setup_only = np.concatenate([Fm["w1"].transpose(2, 0, 1).reshape(C, E * C), expand.reshape(B * H, B * C),
                                 np.broadcast_to(rows[None, :], (128, 4 * C))], axis=1)
    penalty = np.zeros((E, E, C), ml_dtypes.bfloat16)
    for e in range(E):
        penalty[e, e, :] = MASKED
    host = {"x": a["L0_attn_x"], "weights": weights, "vectors": vectors,
            "b2_experts": Fm["b2"], "consts": consts, "setup_only": setup_only, "penalty_rows": penalty.reshape(E, E * C)}

    nc = bacc.Bacc("TRN2", target_bir_lowering=False, num_devices=1)
    arrays, args = {}, []
    for name, array in host.items():
        array = np.ascontiguousarray(array)
        arrays[name] = array
        args.append(nc.dram_tensor(name, array.shape, mybir.dt.from_np(array.dtype), kind="ExternalInput").ap())
    args.append(nc.dram_tensor("out", (B, T, C), F32, kind="ExternalOutput").ap())
    build(nc, *args)
    r = run_bass_kernel_spmd(nc, [arrays], core_ids=[0])
    return r.results[0]["out"]
```

```python
from contextlib import ExitStack

import concourse.bass as bass
from concourse import mybir

ALU = mybir.AluOpType
ACT = mybir.ActivationFunctionType
F32 = mybir.dt.float32
BF16 = mybir.dt.bfloat16
F32R = mybir.dt.float32r
U32 = mybir.dt.uint32
X = mybir.AxisListType.X

B, T, C = 8, 512, 128
TC = 64
NCH = T // TC
N = B * TC
TILES = N // 128
E = 8
H, D = 16, 8
FF = 4
EPS = 1e-5
NEG_INF = -1e38
MASKED = -3e38
EXP_IS_ZERO = -104.0
ATT_SCALE = float(D) ** -0.5

AHEAD = 2
LAST_LAG = 5
SLOTS = NCH + LAST_LAG

VEC = ["w", "u", "g1", "b1", "tmk", "tmv", "tmr", "g2", "b2", "cmk", "cmr", "bq", "bk", "bv", "bo",
       "g3", "b3", "g4", "b4"] + [f"be{e}" for e in range(E)]
VI = {name: i for i, name in enumerate(VEC)}
K_ID, K_CENTRE, K_MEAN, K_HEADS = 0, 128, 256, 384
K_IOTA = K_HEADS + 4 * H
K_RB = K_IOTA + TILES * 2 * E
K_PARTS = K_RB + E
K_HIDE = K_PARTS + 2
K_ALL = K_HIDE + 1
U_W1, U_SPREAD, U_SELECT = 0, E * C, E * C + B * C
U_CM = U_SELECT + TILES * C
U_ROWS = U_CM + FF * C
U_ZERO = U_ROWS + 4 * C
W_TM, W_CP = 0, 3 * C
W_QKV = W_CP + FF * C
W_ROUTER = W_QKV + 3 * C
W_OUT = W_ROUTER + E
W_2 = W_OUT + C
W_ALL = W_2 + E * C


def build(nc, x, weights, vectors, b2_experts, consts, setup_only, penalty_rows, out):
    with ExitStack() as ctx:
        def sb(name, shape, dt=F32):
            return ctx.enter_context(nc.sbuf_tensor(name, shape, dt))

        def bank(name):
            return ctx.enter_context(nc.psum_tensor(name, [128, N], F32))

        def sem(name):
            return ctx.enter_context(nc.semaphore(name))

        wt = sb("wt", [128, W_ALL])
        vec = sb("vec", [128, len(VEC)])
        b2e = sb("b2e", [2 * E, C])
        b2c = sb("b2c", [2 * E, C])
        b2r = sb("b2r", [2 * E, C], F32R)
        wsum = sb("wsum", [128, 1 + E])
        b2sum = sb("b2sum", [2 * E, 1])
        bo_c = sb("bo_c", [128, 1])
        centre_r = sb("centre_r", [128, 128], F32R)
        cst = sb("cst", [128, K_ALL])
        pen = sb("pen", [E, E * C], BF16)
        wrow = sb("wrow", [128, B, TC + 1])
        om = sb("om", [128, 5])
        half_u = sb("half_u", [128, 1])
        eps_c = sb("eps_c", [128, 1])
        ident = cst[:, K_ID:K_ID + 128]
        centre = cst[:, K_CENTRE:K_CENTRE + 128]
        mean = cst[:, K_MEAN:K_MEAN + 128]

        router_bias = cst[:, K_RB:K_RB + E]

        def V(name):
            return vec[:, VI[name]:VI[name] + 1]

        xres = sb("xres", [128, B, T])
        xl = sb("xl", [128, B, T + 1])
        x2 = sb("x2", [128, B, T + 1])

        xtok = sb("xtok", [128, TILES, C])
        stats = sb("stats", [128, TILES, 6])
        mv = sb("mv", [128, TILES, 2])
        ln_v = sb("ln_v", [128, TILES])
        inv_v = sb("inv_v", [128, TILES])
        r1 = sb("r1", [128, TILES])
        q2 = sb("q2", [128, TILES])
        ln_q = sb("ln_q", [128, TILES])
        ln_vq = sb("ln_vq", [128, TILES])
        r12 = sb("r12", [128, TILES])
        xltok = sb("xltok", [128, TILES, C])
        ztok = sb("ztok", [128, TILES, C])
        z = sb("z", [128, N])
        vv = sb("vv", [128, B, TC])
        rr = sb("rr", [128, B, TC])
        kx = sb("kx", [128, B, TC + 1])
        mx = sb("mx", [128, B, TC + 1])
        ax = sb("ax", [128, B, TC + 1])
        bx = sb("bx", [128, B, TC + 1])
        dx = sb("dx", [128, B, TC + 1])
        bbx = sb("bbx", [128, B, TC + 1])
        dl = sb("dl", [128, B, TC])
        alx = sb("alx", [128, B, TC + 1])
        bvx = sb("bvx", [128, B, TC + 1])
        aax = sb("aax", [128, B, TC + 1])
        df = sb("df", [128, B, TC])

        sqr = {s: sb("sqr_" + s, [128, N]) for s in "cahe"}
        log_v, r, r_hi = (
            {s: sqr[s][:, 128 * i:128 * i + 128].bitcast(dt) for s in "cahe"}
            for i, dt in enumerate((F32, F32, F32R)))
        r_parts = {s: sb("r_parts_" + s, [128, 128], F32R)[:, :] for s in "cahe"}
        select = sb("select", [128, TILES, 128], F32R)

        xn = sb("xn", [128, N])
        xg = sb("xg", [128, N])
        xg2 = sb("xg2", [128, 2, N], F32R)
        wcm2 = sb("wcm2", [128, 2, FF * C], F32R)
        xpk = sb("xpk", [128, B, TC])
        xpr = sb("xpr", [128, B, TC])
        kk = sb("kk", [128, 2, N])
        kk2 = sb("kk2", [128, FF, N])
        xs = sb("xs", [128, B, TC])

        x3 = sb("x3", [128, N])
        qkv = sb("qkv", [128, 3, N])
        prod = sb("prod", [128, B, N])
        boot = prod[:, :, :].rearrange("p s n -> p (s n)")
        pr = sb("pr", [128, TILES, B, H])
        smax = sb("smax", [128, TILES, H])
        ssum = sb("ssum", [128, TILES, H])
        sinv = sb("sinv", [128, TILES, H])
        st = sb("st", [128, N])
        attn = sb("attn", [128, 2, N], F32R)
        spread = sb("spread", [128, B * C], F32R)
        y4 = sb("y4", [128, N])
        h = sb("h", [128, N])
        h2 = sb("h2", [128, 2, N], F32R)
        w1 = sb("w1", [128, 2, E * C], F32R)
        lg = sb("lg", [128, TILES, E])
        lmax = sb("lmax", [128, TILES])
        top = sb("top", [128, TILES, 8])
        topi = sb("topi", [128, TILES, 8], U32)
        assign = sb("assign", [128, TILES])
        mask = sb("mask", [128, TILES, 2 * E], BF16)
        ident16 = sb("ident16", [128, 128], BF16)
        maskt = sb("maskt", [2 * E, N], F32R)
        unmask = sb("unmask", [E, N], BF16)

        he = sb("he", [128, 2, N])
        fo = sb("fo", [128, B, TC])
        otok = sb("otok", [128, TILES, C])

        pA, pB, pC = [bank("pA0"), bank("pA1")], [bank("pB0"), bank("pB1")], [bank("pC0"), bank("pC1")]
        pAcc, pMoe = bank("pAcc"), bank("pMoe")

        s_load_tm = sem("s_load_tm")
        s_load_rest = sem("s_load_rest")
        s_const = sem("s_const")
        s_const_w = sem("s_const_w")
        s_bo = sem("s_bo")
        s_pool0 = sem("s_pool0")
        s_passed_dve, s_passed_pool = sem("s_passed_dve"), sem("s_passed_pool")
        s_x = sem("s_x")
        s_stats, s_mv, s_r1, s_q2, s_lnq, s_lnvq, s_r12 = (
            sem(n) for n in ("s_stats", "s_mv", "s_r1", "s_q2", "s_lnq", "s_lnvq", "s_r12"))
        s_norm = sem("s_norm")
        s_xT, s_xlT, s_zT = sem("s_xT"), sem("s_xlT"), sem("s_zT")
        s_xTe, s_xlTe, s_zTe = sem("s_xTe"), sem("s_xlTe"), sem("s_zTe")
        s_prev0 = sem("s_prev0")
        s_kps, s_vps, s_rps = sem("s_kps"), sem("s_vps"), sem("s_rps")
        s_k, s_v, s_r = sem("s_k"), sem("s_v"), sem("s_r")
        s_m, s_kcarry = sem("s_m"), sem("s_kcarry")
        s_am, s_bm, s_ab = sem("s_am"), sem("s_bm"), sem("s_ab")
        s_d, s_dcarry, s_lnd = sem("s_d"), sem("s_dcarry"), sem("s_lnd")
        s_bb, s_dl, s_t12, s_alpha = sem("s_bb"), sem("s_dl"), sem("s_t12"), sem("s_alpha")
        s_bv, s_aa, s_aacarry, s_df = sem("s_bv"), sem("s_aa"), sem("s_aacarry"), sem("s_df")
        s_th, s_ysteps, s_x2 = sem("s_th"), sem("s_ysteps"), sem("s_x2")
        s_wrap = sem("s_wrap")
        s_cen = {s: sem("s_cen_" + s) for s in "ca"}
        s_kept = {s: sem("s_kept_" + s) for s in "cae"}
        s_sq = {s: sem("s_sq_" + s) for s in "cahe"}
        s_var = {s: sem("s_var_" + s) for s in "cahe"}
        s_lnr = {s: sem("s_lnr_" + s) for s in "cahe"}
        s_re = {s: sem("s_re_" + s) for s in "cahe"}
        s_parts = {s: sem("s_parts_" + s) for s in "cahe"}
        s_rstd = {s: sem("s_rstd_" + s) for s in "cahe"}
        s_nrm = {s: sem("s_nrm_" + s) for s in "cahe"}
        s_xn, s_xp, s_xhi, s_xlo = sem("s_xn"), sem("s_xp"), sem("s_xhi"), sem("s_xlo")
        s_kk, s_kkm, s_kk2 = sem("s_kk"), sem("s_kkm"), sem("s_kk2")
        s_vvps, s_tr, s_thc, s_o1, s_xs, s_xres = (
            sem(n) for n in ("s_vvps", "s_tr", "s_thc", "s_o1", "s_xs", "s_xres"))
        s_qkvps, s_qkv = sem("s_qkvps"), sem("s_qkv")
        s_prod, s_score = sem("s_prod"), sem("s_score")
        s_st, s_sT, s_ahi = sem("s_st"), sem("s_sT"), sem("s_ahi")
        s_hhi, s_hlo = sem("s_hhi"), sem("s_hlo")
        s_smax, s_sm, s_pr, s_ssum, s_sinv, s_a = (
            sem(n) for n in ("s_smax", "s_sm", "s_pr", "s_ssum", "s_sinv", "s_a"))
        s_aT, s_attn = sem("s_aT"), sem("s_attn")
        s_exp, s_pv = sem("s_exp"), sem("s_pv")
        s_add, s_ops, s_y4 = sem("s_add"), sem("s_ops"), sem("s_y4")
        s_h, s_lgps, s_top = sem("s_h"), sem("s_lgps"), sem("s_top")
        s_lgsteps = sem("s_lgsteps")
        s_assign, s_mask, s_maskps, s_maskt = (
            sem(n) for n in ("s_assign", "s_mask", "s_maskps", "s_maskt"))
        s_pre, s_he, s_moe = sem("s_pre"), sem("s_he"), sem("s_moe")
        s_fa, s_fo, s_oT, s_otok = sem("s_fa"), sem("s_fo"), sem("s_oT"), sem("s_otok")
        s_out = sem("s_out")

        def v3(ap):
            return ap.rearrange("p (b t) -> p b t", b=B)

        def cols(first, j):
            if isinstance(j, int):
                return slice(first + (j + 1) % NCH * TC, first + (j + 1) % NCH * TC + TC)
            return bass.ds(j * TC + (first + TC), TC)

        def cols_tm(first, n):
            if isinstance(n, int):
                return slice(first + n * TC, first + n * TC + TC)
            return bass.ds(n * TC + first, TC)

        def after(eng, s, count):
            if not isinstance(count, int) or count > 0:
                eng.wait_ge(s, count)

        def own_wait(eng, passed):
            eng.sem_inc(passed, 1)

        def active(s, lag):
            return not isinstance(s, int) or lag <= s < lag + NCH

        def slot_steps(s):
            def go(step, lag, *which):
                if active(s, lag):
                    step(s - lag, *which)
            return go

        def run_slots(eng, slot):
            for s in range(LAST_LAG + 1):
                slot(s)
            with eng.Fori(LAST_LAG + 1, NCH) as s:
                slot(s)
            for s in range(NCH, SLOTS):
                slot(s)

        LOADS_TM, LOADS_REST = 4, 8
        SETUP_TM, SETUP_CM, SETUP_OUT, SETUP_ALL = 3, 5, 9, 13
        block = ctx.enter_context(nc.Block())

        @block.sync
        def _(sp):
            x_rows = x.rearrange("(j b) t c -> b t j c", b=2)
            o_rows = out.rearrange("(j b) t c -> b t j c", b=2)

            def load_x(n):
                after(sp, s_norm, n)
                after(sp, s_xT, n)
                for half in range(2):
                    sp.dma_start(xtok[TC * half:TC * half + TC, :, :],
                                 x_rows[half, cols_tm(0, n)]).then_inc(s_x, 16)

            def store(j):
                sp.wait_ge(s_otok, j + 1)
                for half in range(2):
                    sp.dma_start(o_rows[half, cols(0, j)],
                                 otok[TC * half:TC * half + TC, :, :]).then_inc(s_out, 16)

            load_x(0)
            U_CMK = U_ROWS + 3 * C
            sp.dma_start(cst[:, K_ID:K_CENTRE], consts[:, K_ID:K_CENTRE]).then_inc(s_load_tm, 16)
            sp.dma_start(vec[:, :], vectors).then_inc(s_load_tm, 16)
            sp.dma_start(boot[:, U_ROWS:U_CMK], setup_only[:, U_ROWS:U_CMK]).then_inc(s_load_tm, 16)
            sp.dma_start(wt[:, 0:W_CP], weights[:, 0:W_CP]).then_inc(s_load_tm, 16)
            sp.dma_start(cst[:, K_CENTRE:K_ALL], consts[:, K_CENTRE:K_ALL]).then_inc(s_load_rest, 16)
            sp.dma_start(boot[:, U_CMK:U_ZERO], setup_only[:, U_CMK:U_ZERO]).then_inc(s_load_rest, 16)
            sp.dma_start(wt[:, W_CP:W_QKV], weights[:, W_CP:W_QKV]).then_inc(s_load_rest, 16)
            sp.dma_start(wt[:, W_QKV:W_OUT], weights[:, W_QKV:W_OUT]).then_inc(s_load_rest, 16)
            sp.dma_start(boot[:, 0:U_ROWS], setup_only[:, 0:U_ROWS]).then_inc(s_load_rest, 16)
            sp.dma_start(wt[:, W_OUT:W_ALL], weights[:, W_OUT:W_ALL]).then_inc(s_load_rest, 16)
            sp.dma_start(b2e[:, :], b2_experts).then_inc(s_load_rest, 16)
            sp.dma_start(pen[:, :], penalty_rows).then_inc(s_load_rest, 16)

            def slot(s):
                if active(s, 0) and not (isinstance(s, int) and s == 0):
                    load_x(s)
                if active(s, LAST_LAG):
                    store(s - LAST_LAG)

            run_slots(sp, slot)
            sp.wait_ge(s_out, 32 * NCH)

        @block.gpsimd
        def _(pool):
            g = nc.gpsimd
            g.memset(kx[:, :, 0:1], NEG_INF)
            g.memset(ax[:, :, 0:1], 0.0)
            g.memset(bx[:, :, 0:1], 1.0)
            g.memset(alx[:, :, 0:1], 0.0)
            g.memset(bvx[:, :, 0:1], 0.0)
            g.memset(wrow[:, :, 0:1], NEG_INF)
            g.memset(eps_c[:, :], EPS).then_inc(s_pool0, 1)
            pool.wait_ge(s_load_tm, 16 * LOADS_TM)

            def tm_m(n):
                pool.wait_ge(s_m, n + 1)
                after(pool, s_d, n)
                g.tensor_tensor(ax[:, :, 1:TC + 1], mx[:, :, 0:TC], mx[:, :, 1:TC + 1], ALU.subtract).then_inc(s_am, 1)
                g.tensor_tensor(bx[:, :, 1:TC + 1], kx[:, :, 1:TC + 1], mx[:, :, 1:TC + 1], ALU.subtract).then_inc(s_bm, 1)
                g.tensor_copy(kx[:, :, 0:1], mx[:, :, TC:TC + 1]).then_inc(s_kcarry, 1)

            def tm_bb(n):
                pool.wait_ge(s_d, n + 1)
                own_wait(pool, s_passed_pool)
                g.tensor_copy(bx[:, :, 0:1], dx[:, :, TC:TC + 1]).then_inc(s_dcarry, 1)
                pool.wait_ge(s_lnd, n + 1)
                g.tensor_tensor(bbx[:, :, :], bbx[:, :, :], mx[:, :, :], ALU.add).then_inc(s_bb, 1)
                pool.wait_ge(s_bb, n + 1)
                after(pool, s_th, n)
                after(pool, s_t12, n)
                g.tensor_tensor(dl[:, :, :], bbx[:, :, 0:TC], kx[:, :, 1:TC + 1], ALU.subtract).then_inc(s_dl, 1)

            def tm_bv(n):
                pool.wait_ge(s_alpha, n + 1)
                pool.wait_ge(s_v, n + 1)
                g.tensor_tensor(bvx[:, :, 1:TC + 1], bvx[:, :, 1:TC + 1], vv[:, :, :], ALU.mult).then_inc(s_bv, 1)

            def tm_df(n):
                pool.wait_ge(s_aa, n + 1)
                after(pool, s_x2, n)
                g.tensor_tensor(df[:, :, :], aax[:, :, 0:TC], vv[:, :, :], ALU.subtract).then_inc(s_df, 1)
                g.tensor_copy(bvx[:, :, 0:1], aax[:, :, TC:TC + 1]).then_inc(s_aacarry, 1)

            def ln_parts(j, st):
                pool.wait_ge(s_re[st], j + 1)
                g.tensor_tensor(r_parts[st], r[st], r_hi[st], ALU.subtract).then_inc(s_parts[st], 1)

            def cm_xn(j):
                pool.wait_ge(s_nrm["c"], j + 1)
                after(pool, s_tr, j)
                own_wait(pool, s_passed_pool)
                g.tensor_scalar(xg[:, :], xn[:, :], V("g2"), V("b2"), ALU.mult, ALU.add).then_inc(s_xn, 1)

            def cm_xlo(j):
                pool.wait_ge(s_xhi, j + 1)
                pool.wait_ge(s_xn, j + 1)
                g.tensor_tensor(xg2[:, 1, :], xg[:, :], xg2[:, 0, :], ALU.subtract).then_inc(s_xlo, 1)

            def cm_xs(j):
                pool.wait_ge(s_x2, (j + 2) if not isinstance(j, int) else min(j + 2, NCH))
                after(pool, s_xres, j)
                g.tensor_tensor(xs[:, :, :], xres[:, :, cols(0, j)], x2[:, :, cols(1, j)], ALU.add).then_inc(s_xs, 1)

            def at_add(j, step):
                if step < 4:
                    pool.wait_ge(s_pv, 8 * j + 2 * step + 2)
                    a, b = prod[:, 2 * step, :], prod[:, 2 * step + 1, :]
                elif step == 4:
                    pool.wait_ge(s_add, 6 * j + 4)
                    p4 = prod[:, :, :].rearrange("p (u w) n -> p u w n", w=4)
                    a, b = p4[:, :, 0, :], p4[:, :, 2, :]
                else:
                    pool.wait_ge(s_add, 6 * j + 5)
                    a, b = prod[:, 0, :], prod[:, 4, :]
                g.tensor_tensor(a, a, b, ALU.add).then_inc(s_add, 1)

            def at_h(j):
                pool.wait_ge(s_nrm["h"], j + 1)
                after(pool, s_lgps, j)
                after(pool, s_hlo, j)
                own_wait(pool, s_passed_pool)
                g.tensor_scalar(h[:, :], y4[:, :], V("g3"), V("b3"), ALU.mult, ALU.add).then_inc(s_h, 1)

            def at_hlo(j):
                pool.wait_ge(s_hhi, j + 1)
                pool.wait_ge(s_h, j + 1)
                g.tensor_tensor(h2[:, 1, :], h[:, :], h2[:, 0, :], ALU.subtract).then_inc(s_hlo, 1)

            def ex_out(j):
                pool.wait_ge(s_fa, j + 1)
                g.tensor_tensor(fo[:, :, :], fo[:, :, :], xres[:, :, cols(0, j)], ALU.add).then_inc(s_fo, 1)

            def slot(s):
                go = slot_steps(s)
                go(at_hlo, 5)
                go(cm_xn, 3)
                go(cm_xlo, 3)
                go(tm_m, 1)
                go(tm_bb, 1)
                go(at_add, 4, 0)
                go(cm_xs, 3)
                go(at_add, 4, 1)
                go(tm_bv, 1)
                go(at_add, 4, 2)
                go(tm_df, 1)
                go(at_add, 4, 3)
                go(at_add, 4, 4)
                go(ln_parts, 5, "e")
                go(at_add, 4, 5)
                go(ex_out, 5)
                go(ln_parts, 3, "a")
                go(ln_parts, 2, "c")
                go(ln_parts, 4, "h")
                go(at_h, 4)

            run_slots(pool, slot)

        @block.scalar
        def _(act):
            a = nc.scalar
            eps = eps_c[:, 0:1]
            GELU_TANH, EXP_LN = "gelu_and_others", "natural_log_exp_and_others"
            loaded = [None]

            def table(functions):
                if loaded[0] != functions:
                    loaded[0] = functions
                    a.preload_act_table_set(functions)

            table(EXP_LN)
            act.wait_ge(s_pool0, 1)

            def tm_stats(n):
                table(EXP_LN)
                act.wait_ge(s_mv, n + 1)
                a.activation(ln_v[:, :], mv[:, :, 1], ACT.Ln, bias=eps).then_inc(s_r1, 1)
                act.wait_ge(s_r1, 3 * n + 1)
                after(act, s_norm, n)
                a.activation(inv_v[:, :], ln_v[:, :], ACT.Exp, scale=-1.0).then_inc(s_r1, 1)
                a.activation(r1[:, :], ln_v[:, :], ACT.Exp, scale=-0.5).then_inc(s_r1, 1)
                act.wait_ge(s_q2, n + 1)
                a.activation(ln_q[:, :], q2[:, :], ACT.Ln, bias=eps).then_inc(s_lnq, 1)
                act.wait_ge(s_lnvq, n + 1)
                a.activation(r12[:, :], ln_vq[:, :], ACT.Exp, scale=-0.5).then_inc(s_r12, 1)

            def tm_evac(n):
                if isinstance(n, int) and n == 0:
                    act.wait_ge(s_load_tm, 16 * LOADS_TM)
                    act.wait_ge(s_const, SETUP_TM)
                act.wait_ge(s_xT, n + 1)
                a.copy(xres[:, :, cols_tm(0, n)], v3(pA[0][:, :])).then_inc(s_xTe, 1)
                act.wait_ge(s_xlT, n + 1)
                a.copy(xl[:, :, cols_tm(1, n)], v3(pA[1][:, :])).then_inc(s_xlTe, 1)
                if isinstance(n, int) and n == 0:
                    a.copy(xl[:, :, 0:1], v3(pA[1][:, :])[:, :, 0:1]).then_inc(s_prev0, 1)
                act.wait_ge(s_zT, n + 1)
                after(act, s_rps, n)
                a.activation(z[:, :], pA[0][:, :], ACT.Identity, scale=V("g1"), bias=V("b1")).then_inc(s_zTe, 1)

            def tm_ab(n):
                table(EXP_LN)
                act.wait_ge(s_am, n + 1)
                a.activation(ax[:, :, 1:TC + 1], ax[:, :, 1:TC + 1], ACT.Exp, bias=V("w"))
                act.wait_ge(s_bm, n + 1)
                a.activation(bx[:, :, 1:TC + 1], bx[:, :, 1:TC + 1], ACT.Exp).then_inc(s_ab, 1)

            def tm_lnd(n):
                table(EXP_LN)
                act.wait_ge(s_d, n + 1)
                after(act, s_dl, n)
                a.activation(bbx[:, :, :], dx[:, :, :], ACT.Ln).then_inc(s_lnd, 1)

            def tm_alpha(n):
                table(EXP_LN)
                act.wait_ge(s_t12, n + 1)
                a.activation(alx[:, :, 1:TC + 1], alx[:, :, 1:TC + 1], ACT.Exp)
                a.activation(bvx[:, :, 1:TC + 1], bvx[:, :, 1:TC + 1], ACT.Exp, scale=-1.0).then_inc(s_alpha, 1)

            def tm_tanh(n):
                table(GELU_TANH)
                act.wait_ge(s_t12, n + 1)
                act.wait_ge(s_dl, n + 1)
                a.activation(dl[:, :, :], dl[:, :, :], ACT.Tanh, scale=0.5, bias=half_u[:, 0:1])
                act.wait_ge(s_r, n + 1)
                a.activation(rr[:, :, :], rr[:, :, :], ACT.Tanh, scale=0.5).then_inc(s_th, 1)

            centred = {"c": (pA[0], s_cen["c"], 1), "a": (pB[0], s_cen["a"], 1), "h": (y4, s_y4, 1),
                       "e": (pMoe, s_moe, E)}
            variance = {"c": pA[1], "a": pB[1], "h": pC[1], "e": pC[1]}

            def ln_square(j, st):
                src, complete, per_chunk = centred[st]
                act.wait_ge(complete, per_chunk * j + per_chunk)
                after(act, s_nrm[st], j)
                a.activation(sqr[st][:, :], src[:, :], ACT.Square).then_inc(s_sq[st], 1)

            def ln_keep(j, st):
                src, complete, per_chunk = centred[st]
                act.wait_ge(complete, per_chunk * j + per_chunk)
                if st == "c":
                    after(act, s_xn, j)
                    after(act, s_xhi, j)
                    a.copy(xn[:, :], src[:, :]).then_inc(s_kept[st], 1)
                elif st == "a":
                    after(act, s_y4, j)
                    a.copy(x3[:, :], src[:, :]).then_inc(s_kept[st], 1)
                else:
                    after(act, s_oT, j)
                    a.copy(fo[:, :, :], v3(src[:, :])).then_inc(s_kept[st], 1)

            def ln_rstd(j, st):
                table(EXP_LN)
                act.wait_ge(s_var[st], j + 1)
                a.activation(log_v[st], variance[st][:, 0:128], ACT.Ln, bias=eps).then_inc(s_lnr[st], 1)
                act.wait_ge(s_lnr[st], j + 1)
                a.activation(r[st], log_v[st], ACT.Exp, scale=-0.5)
                a.activation(r_hi[st], log_v[st], ACT.Exp, scale=-0.5,
                             bias=cst[:, K_HIDE:K_HIDE + 1]).then_inc(s_re[st], 1)

            def cm_xhi(j):
                act.wait_ge(s_nrm["c"], j + 1)
                after(act, s_kk, 4 * j)
                a.activation(xg2[:, 0, :], xn[:, :], ACT.Identity, scale=V("g2"), bias=V("b2")).then_inc(s_xhi, 1)

            def cm_tanh(j):
                table(GELU_TANH)
                act.wait_ge(s_tr, j + 1)
                a.activation(xpr[:, :, :], xpr[:, :, :], ACT.Tanh, scale=0.5).then_inc(s_thc, 1)

            def at_qkv(j, i):
                act.wait_ge(s_qkvps, 3 * j + i + 1)
                if i < 2:
                    after(act, s_prod, 4 * j)
                else:
                    after(act, s_pv, 8 * j)
                a.activation(qkv[:, i, :], pB[i % 2][:, :] if i else pB[0][:, :], ACT.Identity,
                             bias=V(("bq", "bk", "bv")[i])).then_inc(s_qkv, 1)

            def at_exp(j):
                table(EXP_LN)
                act.wait_ge(s_sm, j + 1)
                a.activation(pr[:, :, :, :], pr[:, :, :, :], ACT.Exp, scale=ATT_SCALE).then_inc(s_pr, 1)

            def at_st(j):
                act.wait_ge(s_score, j + 1)
                after(act, s_sT, j)
                a.copy(st[:, :], pB[1][:, :]).then_inc(s_st, 1)

            def at_attn(j):
                act.wait_ge(s_aT, j + 1)
                after(act, s_exp, 8 * j)
                after(act, s_attn, j)
                a.copy(attn[:, 0, :], pB[1][:, :]).then_inc(s_ahi, 1)

            def at_hhi(j):
                act.wait_ge(s_nrm["h"], j + 1)
                after(act, s_moe, 8 * j)
                a.activation(h2[:, 0, :], y4[:, :], ACT.Identity, scale=V("g3"), bias=V("b3")).then_inc(s_hhi, 1)

            def at_mask(j):
                act.wait_ge(s_maskps, j + 1)
                after(act, s_moe, 8 * j)
                rows = pC[1][:, :].bitcast(BF16)
                a.copy(maskt[:, :], rows[0:2 * E, 0:N])
                a.activation(unmask[:, :], rows[0:E, 0:N], ACT.Identity, scale=-1.0,
                             bias=1.0).then_inc(s_maskt, 1)

            def ex_gelu(j, e):
                table(GELU_TANH)
                act.wait_ge(s_pre, 8 * j + e + 1)
                after(act, s_moe, 8 * j + e - 1)
                a.activation(he[:, e % 2, :], pC[e % 2][:, :], ACT.Gelu, bias=V(f"be{e}")).then_inc(s_he, 1)

            def ex_affine(j):
                act.wait_ge(s_nrm["e"], j + 1)
                a.activation(fo[:, :, :], fo[:, :, :], ACT.Identity, scale=V("g4"), bias=V("b4")).then_inc(s_fa, 1)

            def ex_store(j):
                act.wait_ge(s_oT, j + 1)
                after(act, s_out, 32 * j)
                a.copy(otok[:, :, :], pC[0][:, :].rearrange("p (j c) -> p j c", c=C)).then_inc(s_otok, 1)

            def slot(s):
                go = slot_steps(s)
                go(ln_keep, 5, "e")
                go(tm_stats, 0)
                go(ln_square, 2, "c")
                go(ln_square, 3, "a")
                go(ex_affine, 5)
                go(ln_rstd, 3, "a")
                go(ln_rstd, 2, "c")
                go(ln_square, 4, "h")
                go(ln_keep, 3, "a")
                go(ln_rstd, 4, "h")
                go(ln_keep, 2, "c")
                go(ex_store, 5)
                go(at_qkv, 3, 0)
                go(cm_xhi, 2)
                go(at_qkv, 3, 1)
                go(tm_evac, 0)
                go(at_hhi, 4)
                go(at_qkv, 3, 2)
                go(at_mask, 4)
                go(ex_gelu, 4, 0)
                go(at_st, 3)
                go(ex_gelu, 4, 1)
                go(at_exp, 3)
                go(tm_ab, 0)
                go(ex_gelu, 4, 2)
                go(ex_gelu, 4, 3)
                go(at_attn, 3)
                go(tm_lnd, 0)
                go(ex_gelu, 4, 4)
                go(ex_gelu, 4, 5)
                go(tm_alpha, 0)
                go(ex_gelu, 4, 6)
                go(cm_tanh, 2)
                go(ex_gelu, 4, 7)
                go(tm_tanh, 0)
                go(ln_square, 4, "e")
                go(ln_rstd, 4, "e")

            run_slots(act, slot)

        @block.vector
        def _(dve):
            v = nc.vector

            def statistics(n):
                dve.wait_ge(s_x, 32 * n + 32)
                for i in range(TILES):
                    ins = v.bn_stats(stats[:, i, :], xtok[:, i, :])
                ins.then_inc(s_stats, 1)
                dve.wait_ge(s_stats, n + 1)
                own_wait(dve, s_passed_dve)
                for i in range(TILES):
                    ins = v.bn_aggr(mv[:, i, :], stats[:, i, :])
                ins.then_inc(s_mv, 1)

            statistics(0)
            dve.wait_ge(s_load_tm, 16 * LOADS_TM)
            dve.wait_ge(s_pool0, 1)
            v.memset(boot[:, U_ZERO:U_ZERO + N], 0.0)
            v.tensor_scalar(om[:, 0:3], vec[:, VI["tmk"]:VI["tmk"] + 3], -1.0, 1.0, ALU.mult, ALU.add)
            v.tensor_scalar(om[:, 3:5], vec[:, VI["cmk"]:VI["cmk"] + 2], -1.0, 1.0, ALU.mult, ALU.add)
            v.tensor_scalar(half_u[:, :], V("u"), -0.5, None, ALU.mult).then_inc(s_const, 1)
            v.tensor_tensor(wt[:, W_TM:W_TM + 3 * C], wt[:, W_TM:W_TM + 3 * C], boot[:, U_ROWS:U_ROWS + 3 * C],
                            ALU.mult).then_inc(s_const, 1)
            dve.wait_ge(s_const, 1)
            v.tensor_scalar(wrow[:, :, 1:TC + 1], v3(boot[:, U_ZERO:U_ZERO + N]), V("w"), None, ALU.add).then_inc(s_const, 1)
            dve.wait_ge(s_const, SETUP_TM)

            def first_only(set_up):
                def step(n):
                    if isinstance(n, int) and n == 0:
                        set_up()
                step.__name__ = set_up.__name__
                return step

            @first_only
            def setup_cm():
                dve.wait_ge(s_load_rest, 16 * LOADS_REST)
                hidden = boot[:, U_CM:U_ROWS]
                v.tensor_tensor(hidden.rearrange("p (f c) -> p f c", f=FF), hidden.rearrange("p (f c) -> p f c", f=FF),
                                boot[:, U_ROWS + 3 * C:U_ROWS + 4 * C].unsqueeze(1).broadcast_to([128, FF, C]),
                                ALU.mult).then_inc(s_const_w, 1)
                v.tensor_copy(select[:, :, :], boot[:, U_SELECT:U_CM].rearrange("p (i c) -> p i c", c=C))
                v.tensor_copy(centre_r[:, :], centre)
                v.tensor_copy(ident16[:, :], ident).then_inc(s_const_w, 1)
                v.tensor_copy(spread[:, :], boot[:, U_SPREAD:U_SPREAD + B * C]).then_inc(s_const_w, 1)
                dve.wait_ge(s_const_w, 1)
                v.tensor_copy(wcm2[:, 0, :], hidden).then_inc(s_const_w, 1)
                dve.wait_ge(s_const_w, 4)
                v.tensor_tensor(wcm2[:, 1, :], hidden, wcm2[:, 0, :], ALU.subtract).then_inc(s_const_w, 1)

            @first_only
            def setup_w2():
                blocks = wt[:, W_OUT:W_ALL].rearrange("p (e c) -> p e c", c=C)
                v.tensor_reduce(wsum[:, :], blocks, X, ALU.add).then_inc(s_const_w, 1)
                v.tensor_reduce(b2sum[:, :], b2e[:, :], X, ALU.add).then_inc(s_const_w, 1)
                dve.wait_ge(s_const_w, SETUP_CM + 1)
                v.scalar_tensor_tensor(blocks, wsum[:, :].unsqueeze(2).broadcast_to([128, 1 + E, C]), -1.0 / C,
                                       blocks, ALU.mult, ALU.add).then_inc(s_const_w, 1)
                dve.wait_ge(s_const_w, SETUP_CM + 2)
                v.scalar_tensor_tensor(b2c[:, :], b2sum[:, :].broadcast_to([2 * E, C]), -1.0 / C, b2e[:, :],
                                       ALU.mult, ALU.add).then_inc(s_const_w, 1)

            @first_only
            def setup_w1():
                v.tensor_copy(w1[:, 0, :], boot[:, U_W1:U_W1 + E * C]).then_inc(s_const_w, 1)
                dve.wait_ge(s_const_w, SETUP_OUT)
                v.tensor_copy(b2r[:, :], b2c[:, :]).then_inc(s_const_w, 1)
                dve.wait_ge(s_const_w, SETUP_OUT + 1)
                v.tensor_tensor(w1[:, 1, :], boot[:, U_W1:U_W1 + E * C], w1[:, 0, :], ALU.subtract)
                v.tensor_scalar(b2c[:, :], b2c[:, :], cst[0:2 * E, K_PARTS + 1:K_PARTS + 2], None,
                                ALU.mult).then_inc(s_const_w, 1)
                dve.wait_ge(s_const_w, SETUP_OUT + 3)
                v.scalar_tensor_tensor(b2r[:, :], b2r[:, :], cst[0:2 * E, K_PARTS:K_PARTS + 1], b2c[:, :],
                                       ALU.mult, ALU.add)
                dve.wait_ge(s_bo, 1)
                v.tensor_copy(bo_c[:, :], pAcc[:, 0:1]).then_inc(s_const_w, 1)

            def tm_stats(n):
                if isinstance(n, int) and n == 0:
                    return
                statistics(n)

            def tm_q2(n):
                dve.wait_ge(s_r1, 3 * n + 2)
                v.tensor_tensor(q2[:, :], mv[:, :, 1], inv_v[:, :], ALU.mult).then_inc(s_q2, 1)
                dve.wait_ge(s_lnq, n + 1)
                v.tensor_tensor(ln_vq[:, :], ln_v[:, :], ln_q[:, :], ALU.add).then_inc(s_lnvq, 1)

            def tm_norm(n):
                dve.wait_ge(s_r1, 3 * n + 3)
                dve.wait_ge(s_r12, n + 1)
                after(dve, s_zT, n)
                for i in range(TILES):
                    v.tensor_scalar(xltok[:, i, :], xtok[:, i, :], mv[:, i, 0:1], r1[:, i:i + 1],
                                    ALU.subtract, ALU.mult)
                    ins = v.tensor_scalar(ztok[:, i, :], xtok[:, i, :], mv[:, i, 0:1], r12[:, i:i + 1],
                                          ALU.subtract, ALU.mult)
                ins.then_inc(s_norm, 1)

            def tm_k(n):
                dve.wait_ge(s_xlTe, n + 1)
                dve.wait_ge(s_prev0, 1)
                dve.wait_ge(s_kps, n + 1)
                after(dve, s_dl, n)
                v.scalar_tensor_tensor(kx[:, :, 1:TC + 1], xl[:, :, cols_tm(0, n)], om[:, 0:1], v3(pA[1][:, :]),
                                       ALU.mult, ALU.add).then_inc(s_k, 1)

            def tm_v(n):
                dve.wait_ge(s_vps, n + 1)
                after(dve, s_bv, n)
                after(dve, s_df, n)
                v.scalar_tensor_tensor(vv[:, :, :], xl[:, :, cols_tm(0, n)], om[:, 1:2], v3(pA[0][:, :]),
                                       ALU.mult, ALU.add).then_inc(s_v, 1)

            def tm_r(n):
                dve.wait_ge(s_rps, n + 1)
                v.scalar_tensor_tensor(rr[:, :, :], xl[:, :, cols_tm(0, n)], om[:, 2:3], v3(pA[1][:, :]),
                                       ALU.mult, ALU.add).then_inc(s_r, 1)

            def tm_mscan(n):
                dve.wait_ge(s_k, n + 1)
                after(dve, s_kcarry, n)
                after(dve, s_bb, n)
                after(dve, s_bm, n)
                v.tensor_tensor_scan(mx[:, :, :].rearrange("p b t -> p (b t)"),
                                     wrow[:, :, :].rearrange("p b t -> p (b t)"),
                                     kx[:, :, :].rearrange("p b t -> p (b t)"), NEG_INF,
                                     ALU.add, ALU.max).then_inc(s_m, 1)

            def tm_d(n):
                dve.wait_ge(s_ab, n + 1)
                after(dve, s_dcarry, n)
                after(dve, s_lnd, n)
                v.tensor_tensor_scan(dx[:, :, :].rearrange("p b t -> p (b t)"),
                                     ax[:, :, :].rearrange("p b t -> p (b t)"),
                                     bx[:, :, :].rearrange("p b t -> p (b t)"), 0.0,
                                     ALU.mult, ALU.add).then_inc(s_d, 1)

            def tm_t12(n):
                dve.wait_ge(s_dl, n + 1)
                after(dve, s_aa, n)
                v.tensor_scalar(alx[:, :, 1:TC + 1], dl[:, :, :], V("w"), 0.0, ALU.add, ALU.min)
                v.tensor_scalar(bvx[:, :, 1:TC + 1], dl[:, :, :], V("w"), 0.0, ALU.add, ALU.max).then_inc(s_t12, 1)

            def tm_aa(n):
                dve.wait_ge(s_bv, n + 1)
                after(dve, s_aacarry, n)
                v.tensor_tensor_scan(aax[:, :, :].rearrange("p b t -> p (b t)"),
                                     alx[:, :, :].rearrange("p b t -> p (b t)"),
                                     bvx[:, :, :].rearrange("p b t -> p (b t)"), 0.0,
                                     ALU.mult, ALU.add).then_inc(s_aa, 1)

            def tm_y(n):
                dve.wait_ge(s_df, n + 1)
                dve.wait_ge(s_th, n + 1)
                v.scalar_tensor_tensor(df[:, :, :], dl[:, :, :], 1.0, df[:, :, :],
                                       ALU.add, ALU.mult).then_inc(s_ysteps, 1)
                dve.wait_ge(s_ysteps, 3 * n + 1)
                v.scalar_tensor_tensor(df[:, :, :], vv[:, :, :], 2.0, df[:, :, :],
                                       ALU.mult, ALU.add).then_inc(s_ysteps, 1)
                dve.wait_ge(s_ysteps, 3 * n + 2)
                v.scalar_tensor_tensor(df[:, :, :], rr[:, :, :], 1.0, df[:, :, :],
                                       ALU.add, ALU.mult).then_inc(s_ysteps, 1)
                dve.wait_ge(s_ysteps, 3 * n + 3)
                v.scalar_tensor_tensor(x2[:, :, cols_tm(1, n)], df[:, :, :], 0.25, xl[:, :, cols_tm(1, n)],
                                       ALU.mult, ALU.add).then_inc(s_x2, 1)

            def tm_wrap():
                dve.wait_ge(s_x2, NCH)
                v.tensor_copy(x2[:, :, 0:1], x2[:, :, T:T + 1]).then_inc(s_wrap, 1)

            scales = {"c": pA[1], "a": pB[1], "h": pC[1], "e": pC[1]}

            def ln_scale(st, x, j):
                if st in s_kept:
                    dve.wait_ge(s_kept[st], j + 1)
                dve.wait_ge(s_rstd[st], j + 1)
                v.tensor_tensor(x[:, :], x[:, :], scales[st][:, :], ALU.mult).then_inc(s_nrm[st], 1)

            def cm_scale(j):
                ln_scale("c", xn, j)

            def cm_prev(j):
                if isinstance(j, int) and j == NCH - 1:
                    dve.wait_ge(s_wrap, 1)
                prev = x2[:, :, cols(0, j)]
                after(dve, s_o1, j)
                after(dve, s_kkm, 4 * j)
                v.tensor_scalar(xpk[:, :, :], prev, om[:, 3:4], None, ALU.mult)
                v.tensor_scalar(xpr[:, :, :], prev, om[:, 4:5], None, ALU.mult).then_inc(s_xp, 1)

            def cm_gate(j):
                dve.wait_ge(s_xn, j + 1)
                dve.wait_ge(s_xp, j + 1)
                v.scalar_tensor_tensor(xpr[:, :, :], v3(xg[:, :]), V("cmr"), xpr[:, :, :],
                                       ALU.mult, ALU.add).then_inc(s_tr, 1)

            def cm_hidden(j, f):
                dve.wait_ge(s_kk, 4 * j + f + 1)
                dve.wait_ge(s_xp, j + 1)
                after(dve, s_kk2, 4 * j + f - 1)
                v.tensor_tensor(v3(kk[:, f % 2, :]), v3(pA[f % 2][:, :]), xpk[:, :, :], ALU.add).then_inc(s_kkm, 1)
                dve.wait_ge(s_kkm, 4 * j + f + 1)
                after(dve, s_vvps, j)
                v.scalar_tensor_tensor(kk2[:, f, :], kk[:, f % 2, :], 0.0, kk[:, f % 2, :],
                                       ALU.max, ALU.mult).then_inc(s_kk2, 1)

            def cm_out(j):
                dve.wait_ge(s_thc, j + 1)
                dve.wait_ge(s_vvps, j + 1)
                v.scalar_tensor_tensor(xpr[:, :, :], xpr[:, :, :], 1.0, v3(pAcc[:, :]),
                                       ALU.add, ALU.mult).then_inc(s_o1, 1)
                dve.wait_ge(s_o1, j + 1)
                dve.wait_ge(s_xs, j + 1)
                v.scalar_tensor_tensor(xres[:, :, cols(0, j)], xpr[:, :, :], 0.5, xs[:, :, :],
                                       ALU.mult, ALU.add).then_inc(s_xres, 1)

            def at_scale(j):
                ln_scale("a", x3, j)

            def at_prod(j, i):
                dve.wait_ge(s_qkv, 3 * j + 2)
                after(dve, s_add, 6 * j)
                after(dve, s_ops, j)
                q = v3(qkv[:, 0, :]).unsqueeze(1).broadcast_to([128, 2, B, TC])
                k = v3(qkv[:, 1, :])[:, 2 * i:2 * i + 2, :].unsqueeze(2).broadcast_to([128, 2, B, TC])
                v.tensor_tensor(prod[:, 2 * i:2 * i + 2, :].rearrange("p s (b t) -> p s b t", b=B), q, k,
                                ALU.mult).then_inc(s_prod, 1)

            def at_softmax_in(j):
                dve.wait_ge(s_sT, j + 1)
                S = pB[0][:, :].rearrange("p (j s h) -> p j s h", j=TILES, s=B)
                v.tensor_reduce(smax[:, :, :], S.rearrange("p j s h -> p j h s"), X, ALU.max).then_inc(s_smax, 1)
                dve.wait_ge(s_smax, j + 1)
                after(dve, s_aT, j)
                v.tensor_tensor(pr[:, :, :, :], S, smax[:, :, :].unsqueeze(2).broadcast_to([128, TILES, B, H]),
                                ALU.subtract).then_inc(s_sm, 1)

            def at_softmax_out(j):
                dve.wait_ge(s_pr, j + 1)
                v.tensor_reduce(ssum[:, :, :], pr[:, :, :, :].rearrange("p j s h -> p j h s"), X,
                                ALU.add).then_inc(s_ssum, 1)
                dve.wait_ge(s_ssum, j + 1)
                v.reciprocal(sinv[:, :, :], ssum[:, :, :]).then_inc(s_sinv, 1)
                dve.wait_ge(s_sinv, j + 1)
                v.tensor_tensor(pr[:, :, :, :], pr[:, :, :, :],
                                sinv[:, :, :].unsqueeze(2).broadcast_to([128, TILES, B, H]),
                                ALU.mult).then_inc(s_a, 1)

            def at_alo(j):
                dve.wait_ge(s_ahi, j + 1)
                v.tensor_tensor(attn[:, 1, :], pB[1][:, :], attn[:, 0, :], ALU.subtract).then_inc(s_attn, 1)

            def at_pv(j, s):
                dve.wait_ge(s_exp, 8 * j + s + 1)
                if s == 0:
                    dve.wait_ge(s_qkv, 3 * j + 3)
                val = v3(qkv[:, 2, :])[:, s:s + 1, :].broadcast_to([128, B, TC])
                v.tensor_tensor(v3(prod[:, s, :]), v3(pB[s % 2][:, :]), val, ALU.mult).then_inc(s_pv, 1)

            def at_y(j):
                dve.wait_ge(s_ops, j + 1)
                after(dve, s_h, j)
                after(dve, s_hhi, j)
                v.scalar_tensor_tensor(y4[:, :], pAcc[:, :], bo_c[:, 0:1], x3[:, :], ALU.add, ALU.add).then_inc(s_y4, 1)

            def at_h(j):
                ln_scale("h", y4, j)

            def at_logits(j):
                dve.wait_ge(s_lgps, j + 1)
                v.tensor_tensor(lg[:, :, :], pC[0][:, 0:TILES * E].rearrange("p (j e) -> p j e", e=E),
                                router_bias.unsqueeze(1).broadcast_to([128, TILES, E]),
                                ALU.add).then_inc(s_lgsteps, 1)
                dve.wait_ge(s_lgsteps, 4 * j + 1)
                v.tensor_reduce(lmax[:, :], lg[:, :, :], X, ALU.max).then_inc(s_lgsteps, 1)
                dve.wait_ge(s_lgsteps, 4 * j + 2)
                v.tensor_tensor(lg[:, :, :], lg[:, :, :], lmax[:, :].unsqueeze(2).broadcast_to([128, TILES, E]),
                                ALU.subtract).then_inc(s_lgsteps, 1)
                dve.wait_ge(s_lgsteps, 4 * j + 3)
                v.tensor_scalar(lg[:, :, :], lg[:, :, :], EXP_IS_ZERO, None, ALU.max).then_inc(s_lgsteps, 1)

            def at_route(j):
                dve.wait_ge(s_lgsteps, 4 * j + 4)
                own_wait(dve, s_passed_dve)
                for i in range(TILES):
                    ins = v.max(top[:, i, :], lg[:, i, :])
                ins.then_inc(s_top, 1)
                dve.wait_ge(s_top, 2 * j + 1)
                own_wait(dve, s_passed_dve)
                for i in range(TILES):
                    ins = v.max_index(topi[:, i, :], top[:, i, :], lg[:, i, :])
                ins.then_inc(s_top, 1)
                dve.wait_ge(s_top, 2 * j + 2)
                v.tensor_tensor(assign[:, :], topi[:, :, 0], topi[:, :, 1], ALU.max).then_inc(s_assign, 1)
                dve.wait_ge(s_assign, j + 1)
                after(dve, s_maskps, j)
                v.tensor_tensor(mask[:, :, :], cst[:, K_IOTA:K_RB].rearrange("p (j e) -> p j e", e=2 * E),
                                assign[:, :].unsqueeze(2).broadcast_to([128, TILES, 2 * E]),
                                ALU.is_equal).then_inc(s_mask, 1)

            def ex_scale(j):
                dve.wait_ge(s_kept["e"], j + 1)
                dve.wait_ge(s_rstd["e"], j + 1)
                v.tensor_tensor(fo[:, :, :], fo[:, :, :], v3(scales["e"][:, :]), ALU.mult).then_inc(s_nrm["e"], 1)

            def slot(s):
                go = slot_steps(s)
                go(at_prod, 4, 3)
                go(tm_k, 1)
                go(tm_v, 1)
                go(tm_mscan, 1)
                go(at_softmax_in, 4)
                go(cm_gate, 3)
                go(tm_r, 1)
                go(at_softmax_out, 4)
                go(tm_d, 1)
                go(cm_hidden, 3, 0)
                go(at_alo, 4)
                go(tm_stats, 0)
                go(at_pv, 4, 0)
                go(at_pv, 4, 1)
                go(at_pv, 4, 2)
                if isinstance(s, int) and s == NCH - 1 + 2:
                    tm_wrap()
                go(setup_w1, 2)
                go(at_pv, 4, 3)
                go(tm_t12, 1)
                go(cm_hidden, 3, 1)
                go(at_pv, 4, 4)
                go(at_pv, 4, 5)
                go(setup_cm, 1)
                go(cm_hidden, 3, 2)
                go(at_pv, 4, 6)
                go(tm_aa, 1)
                go(at_pv, 4, 7)
                go(cm_hidden, 3, 3)
                go(tm_y, 1)
                go(cm_out, 3)
                go(tm_q2, 0)
                go(ex_scale, 5)
                go(tm_norm, 0)
                go(at_y, 4)
                go(at_scale, 3)
                go(cm_scale, 2)
                go(at_h, 4)
                go(cm_prev, 2)
                go(at_prod, 3, 0)
                go(setup_w2, 1)
                go(at_logits, 4)
                go(at_route, 4)
                go(at_prod, 3, 1)
                go(at_prod, 3, 2)

            run_slots(dve, slot)

        @block.tensor
        def _(pe):
            t = nc.tensor
            pe.wait_ge(s_load_tm, 16 * LOADS_TM)

            PARTS = ((0, 0), (0, 1), (1, 0))

            def transposes(dst, src, done):
                for i in range(TILES):
                    ins = t.transpose(dst[:, 128 * i:128 * i + 128], src[:, i, :], ident)
                ins.then_inc(done, 1)

            def ln_centre(st, dst, src, j):
                t.matmul(dst, centre, src, start=True, stop=True).then_inc(s_cen[st], 1)

            variance = {"c": pA[1], "a": pB[1], "h": pC[1], "e": pC[1]}

            def ln_var(j, st):
                if st == "h":
                    after(pe, s_nrm["e"], j)
                pe.wait_ge(s_sq[st], j + 1)
                for i in range(TILES):
                    ins = t.matmul(variance[st][32 * i:32 * i + 32, 0:128], mean[:, 0:32],
                                   sqr[st][:, 128 * i:128 * i + 128], start=True, stop=True)
                ins.then_inc(s_var[st], 1)

            def ln_spread(j, st):
                if isinstance(j, int) and j == 0:
                    pe.wait_ge(s_const_w, SETUP_CM)
                pe.wait_ge(s_parts[st], j + 1)
                for i in range(TILES):
                    ins = t.matmul(variance[st][:, 128 * i:128 * i + 128], select[:, i, :], r_parts[st],
                                   start=True, stop=True)
                ins.then_inc(s_rstd[st], 1)

            def setup_bo(n):
                if isinstance(n, int) and n == 0:
                    pe.wait_ge(s_load_rest, 16 * LOADS_REST)
                    t.matmul(pAcc[:, 0:1], centre, V("bo"), start=True, stop=True).then_inc(s_bo, 1)

            def tm_transpose(n, i):
                if i == 0:
                    pe.wait_ge(s_norm, n + 1)
                    if not isinstance(n, int) or n >= AHEAD:
                        pe.wait_ge(s_nrm["c"], n - 1)
                    else:
                        after(pe, s_v, n)
                        after(pe, s_r, n)
                    transposes(pA[0], xtok, s_xT)
                elif i == 1:
                    transposes(pA[1], xltok, s_xlT)
                else:
                    pe.wait_ge(s_xTe, n + 1)
                    transposes(pA[0], ztok, s_zT)

            def tm_kv(n):
                pe.wait_ge(s_zTe, n + 1)
                pe.wait_ge(s_xlTe, n + 1)
                if isinstance(n, int) and n == 0:
                    pe.wait_ge(s_prev0, 1)
                    pe.wait_ge(s_const, SETUP_TM)
                t.matmul(pA[1][:, :], wt[:, W_TM:W_TM + C], z[:, :], start=True, stop=True).then_inc(s_kps, 1)
                t.matmul(pA[0][:, :], wt[:, W_TM + C:W_TM + 2 * C], z[:, :], start=True,
                         stop=True).then_inc(s_vps, 1)

            def tm_r(n):
                pe.wait_ge(s_k, n + 1)
                t.matmul(pA[1][:, :], wt[:, W_TM + 2 * C:W_TM + 3 * C], z[:, :], start=True,
                         stop=True).then_inc(s_rps, 1)

            def cm_centre(j):
                if isinstance(j, int) and j == 0:
                    pe.wait_ge(s_load_rest, 16 * LOADS_REST)
                    pe.wait_ge(s_v, AHEAD)
                    pe.wait_ge(s_r, AHEAD)
                pe.wait_ge(s_x2, (j + 2) if not isinstance(j, int) else min(j + 2, NCH))
                after(pe, s_kkm, 4 * j)
                ln_centre("c", v3(pA[0][:, :]), x2[:, :, cols(1, j)], j)

            def cm_hidden(j, f):
                if f == 0:
                    if isinstance(j, int) and j == 0:
                        pe.wait_ge(s_const_w, SETUP_ALL)
                    pe.wait_ge(s_xlo, j + 1)
                    if not isinstance(j, int) or j + AHEAD < NCH:
                        pe.wait_ge(s_v, j + AHEAD + 1)
                        pe.wait_ge(s_r, j + AHEAD + 1)
                if f >= 2:
                    pe.wait_ge(s_kkm, 4 * j + f - 1)
                for wp, xp in PARTS:
                    ins = t.matmul(pA[f % 2][:, :], wcm2[:, wp, f * C:f * C + C], xg2[:, xp, :], start=(wp + xp == 0),
                                   stop=(wp == 1))
                ins.then_inc(s_kk, 1)

            def cm_mlp(j, f):
                if f == 0:
                    after(pe, s_y4, j - 1)
                    after(pe, s_o1, j)
                pe.wait_ge(s_kk2, 4 * j + f + 1)
                ins = t.matmul(pAcc[:, :], wt[:, W_CP + f * C:W_CP + f * C + C], kk2[:, f, :],
                               start=(f == 0), stop=(f == FF - 1))
                if f == FF - 1:
                    ins.then_inc(s_vvps, 1)

            def at_centre(j):
                pe.wait_ge(s_xres, j + 1)
                after(pe, s_pv, 8 * j)
                ln_centre("a", v3(pB[0][:, :]), xres[:, :, cols(0, j)], j)

            def at_q(j):
                pe.wait_ge(s_nrm["a"], j + 1)
                t.matmul(pB[0][:, :], wt[:, W_QKV:W_QKV + C], x3[:, :], start=True, stop=True).then_inc(s_qkvps, 1)

            def at_kv(j):
                t.matmul(pB[1][:, :], wt[:, W_QKV + C:W_QKV + 2 * C], x3[:, :], start=True,
                         stop=True).then_inc(s_qkvps, 1)
                pe.wait_ge(s_qkv, 3 * j + 1)
                t.matmul(pB[0][:, :], wt[:, W_QKV + 2 * C:W_QKV + 3 * C], x3[:, :], start=True,
                         stop=True).then_inc(s_qkvps, 1)

            def at_scores(j, i):
                pe.wait_ge(s_prod, 4 * j + i + 1)
                for odd in range(2):
                    ins = t.matmul(pB[1][32 * i:32 * i + 32, :],
                                   cst[:, K_HEADS + 2 * H * odd:K_HEADS + 2 * H * odd + 2 * H],
                                   prod[:, 2 * i + odd, :], start=(odd == 0), stop=(odd == 1))
                if i == 3:
                    ins.then_inc(s_score, 1)

            def at_st(j):
                pe.wait_ge(s_st, j + 1)
                pe.wait_ge(s_qkv, 3 * j + 3)
                transposes(pB[0], st[:, :].rearrange("p (j n) -> p j n", n=128), s_sT)

            def at_transpose(j):
                pe.wait_ge(s_a, j + 1)
                transposes(pB[1], pr[:, :, :, :].rearrange("p j s h -> p j (s h)"), s_aT)

            def at_expand(j, s):
                if s == 0:
                    pe.wait_ge(s_attn, j + 1)
                if s >= 2:
                    pe.wait_ge(s_pv, 8 * j + s - 1)
                for part in range(2):
                    ins = t.matmul(pB[s % 2][:, :], spread[:, s * 128:s * 128 + 128], attn[:, part, :],
                                   start=(part == 0), stop=(part == 1))
                ins.then_inc(s_exp, 1)

            def at_out(j):
                pe.wait_ge(s_add, 6 * j + 6)
                if not isinstance(j, int) or j + 1 < NCH:
                    pe.wait_ge(s_o1, j + 2)
                t.matmul(pAcc[:, :], wt[:, W_OUT:W_OUT + C], prod[:, 0, :], start=True, stop=True).then_inc(s_ops, 1)

            def at_router(j):
                pe.wait_ge(s_h, j + 1)
                after(pe, s_otok, j)
                for i in range(TILES):
                    ins = t.matmul(pC[0][:, E * i:E * i + E], h[:, 128 * i:128 * i + 128],
                                   wt[:, W_ROUTER:W_ROUTER + E], start=True, stop=True)
                ins.then_inc(s_lgps, 1)

            def at_mask(j):
                pe.wait_ge(s_mask, j + 1)
                for i in range(TILES):
                    ins = t.transpose(pC[1][:, :].bitcast(BF16)[0:2 * E, 128 * i:128 * i + 128], mask[:, i, :],
                                      ident16[:, :])
                ins.then_inc(s_maskps, 1)

            def ex_in(j, e):
                if e == 0:
                    pe.wait_ge(s_maskt, j + 1)
                    pe.wait_ge(s_hlo, j + 1)
                if e >= 2:
                    pe.wait_ge(s_he, 8 * j + e - 1)
                for wp, hp in PARTS:
                    t.matmul(pC[e % 2][:, :], w1[:, wp, e * C:e * C + C], h2[:, hp, :], start=(wp + hp == 0),
                             stop=False)
                t.matmul(pC[e % 2][:, :], pen[:, e * C:e * C + C], unmask[:, :], start=False,
                         stop=True).then_inc(s_pre, 1)

            def ex_out(j, e):
                pe.wait_ge(s_he, 8 * j + e + 1)
                if e == 0:
                    after(pe, s_nrm["e"], j)
                    for part in range(2):
                        t.matmul(pMoe[:, :], centre_r[:, :], h2[:, part, :], start=(part == 0), stop=False)
                    t.matmul(pMoe[:, :], b2r[:, :], maskt[:, :], start=False, stop=False)
                t.matmul(pMoe[:, :], wt[:, W_2 + e * C:W_2 + e * C + C], he[:, e % 2, :], start=False,
                         stop=(e == E - 1)).then_inc(s_moe, 1)

            def ex_transpose(j):
                pe.wait_ge(s_fo, j + 1)
                transposes(pC[0], fo[:, :, :].rearrange("p (j b) t -> p j (b t)", b=2), s_oT)

            def slot(s):
                go = slot_steps(s)
                go(ln_spread, 5, "h")
                go(at_kv, 4)
                go(tm_transpose, 1, 0)
                go(at_router, 5)
                go(tm_transpose, 1, 1)
                go(tm_transpose, 1, 2)
                go(at_scores, 4, 0)
                go(at_mask, 5)
                go(tm_kv, 1)
                go(ex_in, 5, 0)
                go(ex_in, 5, 1)
                go(at_scores, 4, 1)
                go(at_scores, 4, 2)
                go(at_scores, 4, 3)
                go(ex_in, 5, 2)
                go(at_st, 4)
                go(tm_r, 1)
                go(ex_out, 5, 0)
                go(ex_in, 5, 3)
                go(setup_bo, 2)
                go(cm_hidden, 3, 0)
                go(ex_out, 5, 1)
                go(cm_hidden, 3, 1)
                go(at_transpose, 4)
                go(ex_in, 5, 4)
                go(ex_in, 5, 5)
                go(cm_mlp, 3, 0)
                go(at_expand, 4, 0)
                go(at_expand, 4, 1)
                go(ex_out, 5, 2)
                go(at_expand, 4, 2)
                go(at_expand, 4, 3)
                go(ex_out, 5, 3)
                go(ex_in, 5, 6)
                go(ex_out, 5, 4)
                go(at_expand, 4, 4)
                go(at_expand, 4, 5)
                go(cm_hidden, 3, 2)
                go(ex_out, 5, 5)
                go(at_expand, 4, 6)
                go(ex_in, 5, 7)
                go(at_expand, 4, 7)
                go(cm_hidden, 3, 3)
                go(ex_out, 5, 6)
                go(ex_out, 5, 7)
                go(cm_mlp, 3, 1)
                go(cm_mlp, 3, 2)
                go(ln_var, 5, "e")
                go(cm_mlp, 3, 3)
                go(cm_centre, 2)
                go(ln_spread, 5, "e")
                go(at_centre, 3)
                go(ln_var, 2, "c")
                go(ln_var, 3, "a")
                go(at_out, 4)
                go(ex_transpose, 5)
                go(ln_spread, 3, "a")
                go(ln_var, 4, "h")
                go(ln_spread, 2, "c")
                go(at_q, 3)

            run_slots(pe, slot)


def kernel(**inputs):
    import ml_dtypes
    import numpy as np
    import concourse.bacc as bacc
    from concourse.bass_utils import run_bass_kernel_spmd

    a = {k: np.asarray(v) for k, v in inputs.items()}
    A = {k[8:]: v for k, v in a.items() if k.startswith("L0_attn_")}
    Fm = {k[7:]: v for k, v in a.items() if k.startswith("L0_ffn_")}
    f = np.float32

    weights = np.concatenate([
        A["W_tm"],
        A["W_cp"].reshape(FF, C, C).transpose(1, 0, 2).reshape(C, FF * C),
        Fm["in_proj_w"].T, Fm["router_w"].T, Fm["out_w"].T,
        Fm["w2"].transpose(2, 0, 1).reshape(C, E * C)], axis=1)
    ib = Fm["in_proj_b"].reshape(3, C)
    cols = [A["time_decay"], A["time_first"], A["g1"], A["b1"], A["tmk"].reshape(C), A["tmv"].reshape(C),
            A["tmr"].reshape(C), A["g2"], A["b2"], A["cmk"].reshape(C), A["cmr"].reshape(C),
            ib[0], ib[1], ib[2], Fm["out_b"], Fm["ln1_g"], Fm["ln1_b"], Fm["ln2_g"], Fm["ln2_b"]]
    vectors = np.stack(cols + [Fm["b1"][e] for e in range(E)], axis=1)
    rows = np.concatenate([A["tmk"].reshape(C), A["tmv"].reshape(C), A["tmr"].reshape(C), A["cmk"].reshape(C)])

    eye = np.eye(128, dtype=f)
    average = np.full((128, 128), 1.0 / C, f)
    heads = np.repeat(np.eye(H, dtype=f), D, axis=0)
    iota = np.broadcast_to(np.tile(np.arange(E, dtype=f), 2 * TILES)[None, :], (128, 2 * TILES * E))
    expand = np.zeros((B, H, B, C), f)
    for s in range(B):
        expand[s, :, s, :] = heads.T
    none = np.zeros_like(heads)
    parts = np.zeros((128, 2), f)
    hide = np.zeros((128, 1), f)
    hide[0::2] = -1000.0
    select = np.zeros((128, TILES, C), f)
    for i in range(TILES):
        select[32 * i:32 * i + 2, i, :] = 1.0
    parts[0:E, 0], parts[E:2 * E, 0], parts[E:2 * E, 1] = 1.0, -1.0, 1.0
    consts = np.concatenate([eye, eye - average, average, heads, none, none, heads, iota,
                             np.broadcast_to(Fm["router_b"][None, :], (128, E)), parts, hide], axis=1)
    setup_only = np.concatenate([Fm["w1"].transpose(2, 0, 1).reshape(C, E * C), expand.reshape(B * H, B * C),
                                 select.reshape(128, TILES * C), A["W_cm"],
                                 np.broadcast_to(rows[None, :], (128, 4 * C))], axis=1)
    penalty = np.zeros((E, E, C), ml_dtypes.bfloat16)
    for e in range(E):
        penalty[e, e, :] = MASKED
    host = {"x": a["L0_attn_x"], "weights": weights, "vectors": vectors,
            "b2_experts": np.concatenate([Fm["b2"], Fm["b2"]]), "consts": consts,
            "setup_only": setup_only, "penalty_rows": penalty.reshape(E, E * C)}

    nc = bacc.Bacc("TRN2", target_bir_lowering=False, num_devices=1)
    arrays, args = {}, []
    for name, array in host.items():
        array = np.ascontiguousarray(array)
        arrays[name] = array
        args.append(nc.dram_tensor(name, array.shape, mybir.dt.from_np(array.dtype), kind="ExternalInput").ap())
    args.append(nc.dram_tensor("out", (B, T, C), F32, kind="ExternalOutput").ap())
    build(nc, *args)
    r = run_bass_kernel_spmd(nc, [arrays], core_ids=[0])
    return r.results[0]["out"]
```
